# Optimizing a Trainium2 kernel written in Bass

```python
import numpy as np
import jax
import jax.numpy as jnp

def _softmax(x, axis=-1):
    return jax.nn.softmax(x, axis=axis)

def _gelu(x):
    return jax.nn.gelu(x, approximate=True)

def _silu(x):
    return jax.nn.silu(x)

def _sigmoid(x):
    return jax.nn.sigmoid(x)

def _layernorm(x, axis=-1, eps=1e-05):
    m = jnp.mean(x, axis=axis, keepdims=True)
    v = jnp.var(x, axis=axis, keepdims=True)
    return (x - m) / jnp.sqrt(v + eps)

def _scatter_add(tgt, idx, src, axis=0):
    return tgt.at[idx].add(src)

def _segment_sum(src, seg, n):
    return jax.ops.segment_sum(src, seg, n)
kernel_name = 'mk_seq_preln_d2_jaxref_r4_a6b921'

def setup_inputs(seed: int=0):
    np.random.seed(seed)
    _w = jnp.asarray

    def _L0_attn_setup():
        import jax, jax.numpy as jnp
        import numpy as np
        EPS = 1e-08

        def rms_norm_multihead(x, weight):
            x32 = x.astype(jnp.float32)
            normed = x32 * jax.lax.rsqrt(jnp.mean(x32 * x32, axis=-1, keepdims=True) + EPS)
            return normed.astype(x.dtype) * weight
        key = jax.random.key(seed)
        k0, k1, k2 = jax.random.split(key, 3)
        B, L, D, H = (2, 256, 256, 16)
        d = D // H
        X = jax.random.normal(k0, (B, L, D), dtype=jnp.float32)
        Wq = jax.random.normal(k1, (D, D), dtype=jnp.float32) * 0.02
        Wv = jax.random.normal(k2, (D, D), dtype=jnp.float32) * 0.02
        q_norm_w = jnp.ones((H, d), dtype=jnp.float32)
        v_norm_w = jnp.ones((H, d), dtype=jnp.float32)
        return {'X': X, 'Wq': Wq, 'Wv': Wv, 'q_norm_w': q_norm_w, 'v_norm_w': v_norm_w}
    _L0_attn_in = _L0_attn_setup()

    def _L0_ffn_setup():
        import jax, jax.numpy as jnp
        import numpy as np
        B, S, H = (1, 256, 256)
        E = 256
        NEXP = 16
        TOPK = 2
        ALPHA = 1.702
        LIMIT = 7.0

        def _moe_forward(x, Wg, bg, Wgu, bgu, Wd, bd):
            b, s, h = x.shape
            xt = x.reshape(-1, h)
            logits = xt @ Wg.T + bg
            top_vals, top_idx = jax.lax.top_k(logits, TOPK)
            rw = jax.nn.softmax(top_vals.astype(jnp.float32), axis=-1).astype(xt.dtype)
            onehot = jax.nn.one_hot(top_idx, NEXP, dtype=xt.dtype)
            cw = jnp.einsum('tk,tke->te', rw, onehot)
            gu = jnp.einsum('th,ehf->tef', xt, Wgu) + bgu[None]
            gate = gu[..., ::2]
            up = gu[..., 1::2]
            gate = jnp.minimum(gate, LIMIT)
            up = jnp.clip(up, -LIMIT, LIMIT)
            glu = gate * jax.nn.sigmoid(gate * ALPHA)
            gated = (up + 1.0) * glu
            out_e = jnp.einsum('tef,efh->teh', gated, Wd) + bd[None]
            out = jnp.einsum('teh,te->th', out_e, cw)
            return out.reshape(b, s, h)
        key = jax.random.key(seed)
        ks = jax.random.split(key, 8)
        hidden_states = jax.random.normal(ks[0], (B, S, H), dtype=jnp.float32)
        Wg = jax.random.normal(ks[1], (NEXP, H), dtype=jnp.float32) / np.sqrt(H)
        bg = jax.random.normal(ks[2], (NEXP,), dtype=jnp.float32) * 0.01
        Wgu = jax.random.normal(ks[3], (NEXP, H, 2 * E), dtype=jnp.float32) / np.sqrt(H)
        bgu = jax.random.normal(ks[4], (NEXP, 2 * E), dtype=jnp.float32) * 0.01
        Wd = jax.random.normal(ks[5], (NEXP, E, H), dtype=jnp.float32) / np.sqrt(E)
        bd = jax.random.normal(ks[6], (NEXP, H), dtype=jnp.float32) * 0.01
        return {'hidden_states': hidden_states, 'Wg': Wg, 'bg': bg, 'Wgu': Wgu, 'bgu': bgu, 'Wd': Wd, 'bd': bd}
    _L0_ffn_in = _L0_ffn_setup()

    def _L1_attn_setup():
        import jax, jax.numpy as jnp
        import numpy as np
        B, S, D = (2, 512, 256)
        H, DH = (16, 64)
        DQL, DKVL = (128, 128)
        DR = 64
        TOPK = 64
        LN_EPS = 1e-05
        ROPE_BASE = 10000.0

        def _rope_tables(seq_len, dim):
            inv_freq = 1.0 / ROPE_BASE ** (np.arange(0, dim, 2, dtype=np.float32) / dim)
            t = np.arange(seq_len, dtype=np.float32)
            freqs = np.outer(t, inv_freq)
            cos = np.concatenate([np.cos(freqs), np.cos(freqs)], -1)[:, ::2]
            sin = np.concatenate([np.sin(freqs), np.sin(freqs)], -1)[:, ::2]
            return (jnp.asarray(cos), jnp.asarray(sin))

        def _apply_rope_subspace(x, d_rope):
            s = x.shape[-2]
            cos, sin = _rope_tables(s, d_rope)
            xr, xp = (x[..., :d_rope], x[..., d_rope:])
            e, o = (xr[..., 0::2], xr[..., 1::2])
            rot = jnp.stack([e * cos - o * sin, e * sin + o * cos], axis=-1).reshape(xr.shape)
            return jnp.concatenate([rot, xp], axis=-1)

        def _reference_tuple_inner(x, w_down_q, w_down_kv, w_up_q, w_up_k, w_up_v, w_out, ln_scale, ln_bias):
            b, s, d = x.shape
            residual = x
            mu = jnp.mean(x, axis=-1, keepdims=True)
            var = jnp.mean((x - mu) ** 2, axis=-1, keepdims=True)
            h = (x - mu) * jax.lax.rsqrt(var + LN_EPS) * ln_scale + ln_bias
            c_q = h @ w_down_q.T
            c_kv = h @ w_down_kv.T
            q = (c_q @ w_up_q.T).reshape(b, s, H, DH).transpose(0, 2, 1, 3)
            k = (c_kv @ w_up_k.T).reshape(b, s, H, DH).transpose(0, 2, 1, 3)
            v = (c_kv @ w_up_v.T).reshape(b, s, H, DH).transpose(0, 2, 1, 3)
            q = _apply_rope_subspace(q, DR)
            k = _apply_rope_subspace(k, DR)
            scale = 1.0 / np.sqrt(DH).astype(np.float32)
            scores = jnp.einsum('bhqd,bhkd->bhqk', q, k) * scale
            _, indices = jax.lax.top_k(scores, min(TOPK, s))
            attn = jax.nn.softmax(scores, axis=-1)
            out = jnp.einsum('bhqk,bhkd->bhqd', attn, v)
            out = out.transpose(0, 2, 1, 3).reshape(b, s, H * DH)
            out = out @ w_out.T + residual
            return (out, indices.astype(jnp.int64))
        key = jax.random.key(seed)
        ks = jax.random.split(key, 7)
        init = lambda k, shape: jax.random.normal(k, shape, jnp.float32) * 0.02
        return {'x': jax.random.normal(ks[0], (B, S, D), jnp.float32), 'w_down_q': init(ks[1], (DQL, D)), 'w_down_kv': init(ks[2], (DKVL, D)), 'w_up_q': init(ks[3], (H * DH, DQL)), 'w_up_k': init(ks[4], (H * DH, DKVL)), 'w_up_v': init(ks[5], (H * DH, DKVL)), 'w_out': init(ks[6], (D, H * DH)), 'ln_scale': jnp.ones((D,), jnp.float32), 'ln_bias': jnp.zeros((D,), jnp.float32)}
    _L1_attn_in = _L1_attn_setup()

    def _L1_ffn_setup():
        import jax, jax.numpy as jnp
        import numpy as np
        NUM_EXPERTS = 64
        TOP_K = 8
        HIDDEN = 256
        INTER = 192
        BATCH, SEQ = (1, 256)
        CAPACITY = 64

        def _moe_forward(hidden_states, gate_w, w_gate, w_up, w_down):
            B, S, H = hidden_states.shape
            x = hidden_states.reshape(-1, H)
            T = x.shape[0]
            logits = (x @ gate_w.T).astype(jnp.float32)
            probs = jax.nn.softmax(logits, axis=-1)
            topk_p, topk_i = jax.lax.top_k(probs, TOP_K)
            topk_p = topk_p / jnp.sum(topk_p, axis=-1, keepdims=True)
            flat_e = topk_i.reshape(-1)
            onehot = jax.nn.one_hot(flat_e, NUM_EXPERTS, dtype=jnp.int32)
            pos_all = jnp.cumsum(onehot, axis=0) - 1
            pos = jnp.take_along_axis(pos_all, flat_e[:, None], axis=1)[:, 0]
            x_rep = jnp.repeat(x, TOP_K, axis=0)
            dispatch = jnp.zeros((NUM_EXPERTS, CAPACITY, H), x.dtype)
            dispatch = dispatch.at[flat_e, pos].set(x_rep, mode='drop')
            g = jax.nn.silu(jnp.einsum('ech,eih->eci', dispatch, w_gate))
            u = jnp.einsum('ech,eih->eci', dispatch, w_up)
            y = jnp.einsum('eci,ehi->ech', g * u, w_down)
            valid = pos < CAPACITY
            y_tok = y[flat_e, jnp.minimum(pos, CAPACITY - 1)]
            w = (topk_p.reshape(-1) * valid.astype(topk_p.dtype)).astype(x.dtype)
            out = (y_tok * w[:, None]).reshape(T, TOP_K, H).sum(axis=1)
            return out.reshape(B, S, H)
        key = jax.random.key(seed)
        k1, k2, k3, k4, k5 = jax.random.split(key, 5)
        scale = 0.02
        return {'hidden_states': jax.random.normal(k1, (BATCH, SEQ, HIDDEN), dtype=jnp.float32), 'gate_w': jax.random.normal(k2, (NUM_EXPERTS, HIDDEN), dtype=jnp.float32) * scale, 'w_gate': jax.random.normal(k3, (NUM_EXPERTS, INTER, HIDDEN), dtype=jnp.float32) * scale, 'w_up': jax.random.normal(k4, (NUM_EXPERTS, INTER, HIDDEN), dtype=jnp.float32) * scale, 'w_down': jax.random.normal(k5, (NUM_EXPERTS, HIDDEN, INTER), dtype=jnp.float32) * scale}
    _L1_ffn_in = _L1_ffn_setup()
    _d = {'L0_attn_X': _L0_attn_in['X'], 'L0_attn_Wq': _L0_attn_in['Wq'], 'L0_attn_Wv': _L0_attn_in['Wv'], 'L0_attn_q_norm_w': _L0_attn_in['q_norm_w'], 'L0_attn_v_norm_w': _L0_attn_in['v_norm_w'], 'L0_ffn_Wg': _L0_ffn_in['Wg'], 'L0_ffn_bg': _L0_ffn_in['bg'], 'L0_ffn_Wgu': _L0_ffn_in['Wgu'], 'L0_ffn_bgu': _L0_ffn_in['bgu'], 'L0_ffn_Wd': _L0_ffn_in['Wd'], 'L0_ffn_bd': _L0_ffn_in['bd'], 'L1_attn_w_down_q': _L1_attn_in['w_down_q'], 'L1_attn_w_down_kv': _L1_attn_in['w_down_kv'], 'L1_attn_w_up_q': _L1_attn_in['w_up_q'], 'L1_attn_w_up_k': _L1_attn_in['w_up_k'], 'L1_attn_w_up_v': _L1_attn_in['w_up_v'], 'L1_attn_w_out': _L1_attn_in['w_out'], 'L1_attn_ln_scale': _L1_attn_in['ln_scale'], 'L1_attn_ln_bias': _L1_attn_in['ln_bias'], 'L1_ffn_gate_w': _L1_ffn_in['gate_w'], 'L1_ffn_w_gate': _L1_ffn_in['w_gate'], 'L1_ffn_w_up': _L1_ffn_in['w_up'], 'L1_ffn_w_down': _L1_ffn_in['w_down']}
    _x0 = _d['L0_attn_X']
    _d['L0_attn_X'] = jax.random.normal(jax.random.fold_in(jax.random.key(seed), 1), (2, 2048, 256), dtype=_x0.dtype)
    del _x0
    return _d

def reference(L0_attn_X, L0_attn_Wq, L0_attn_Wv, L0_attn_q_norm_w, L0_attn_v_norm_w, L0_ffn_Wg, L0_ffn_bg, L0_ffn_Wgu, L0_ffn_bgu, L0_ffn_Wd, L0_ffn_bd, L1_attn_w_down_q, L1_attn_w_down_kv, L1_attn_w_up_q, L1_attn_w_up_k, L1_attn_w_up_v, L1_attn_w_out, L1_attn_ln_scale, L1_attn_ln_bias, L1_ffn_gate_w, L1_ffn_w_gate, L1_ffn_w_up, L1_ffn_w_down):

    def _L0_attn_ref(X, Wq, Wv, q_norm_w, v_norm_w):
        import jax, jax.numpy as jnp
        import numpy as np
        EPS = 1e-08

        def rms_norm_multihead(x, weight):
            x32 = x.astype(jnp.float32)
            normed = x32 * jax.lax.rsqrt(jnp.mean(x32 * x32, axis=-1, keepdims=True) + EPS)
            return normed.astype(x.dtype) * weight
        B, L, D = X.shape
        H, d = q_norm_w.shape
        K = X.reshape(B, L, H, d)
        Q = rms_norm_multihead((X @ Wq.T).reshape(B, L, H, d), q_norm_w)
        V = rms_norm_multihead((X @ Wv.T).reshape(B, L, H, d), v_norm_w)
        W = jnp.cumsum(jnp.einsum('blhd,blhe->blhde', K, V), axis=1)
        out = jnp.einsum('blhd,blhde->blhe', Q, W).reshape(B, L, D)
        return out

    def _L0_ffn_ref(hidden_states, Wg, bg, Wgu, bgu, Wd, bd):
        import jax, jax.numpy as jnp
        import numpy as np
        B, S, H = (1, 256, 256)
        E = 256
        NEXP = 16
        TOPK = 2
        ALPHA = 1.702
        LIMIT = 7.0

        def _moe_forward(x, Wg, bg, Wgu, bgu, Wd, bd):
            b, s, h = x.shape
            xt = x.reshape(-1, h)
            logits = xt @ Wg.T + bg
            top_vals, top_idx = jax.lax.top_k(logits, TOPK)
            rw = jax.nn.softmax(top_vals.astype(jnp.float32), axis=-1).astype(xt.dtype)
            onehot = jax.nn.one_hot(top_idx, NEXP, dtype=xt.dtype)
            cw = jnp.einsum('tk,tke->te', rw, onehot)
            gu = jnp.einsum('th,ehf->tef', xt, Wgu) + bgu[None]
            gate = gu[..., ::2]
            up = gu[..., 1::2]
            gate = jnp.minimum(gate, LIMIT)
            up = jnp.clip(up, -LIMIT, LIMIT)
            glu = gate * jax.nn.sigmoid(gate * ALPHA)
            gated = (up + 1.0) * glu
            out_e = jnp.einsum('tef,efh->teh', gated, Wd) + bd[None]
            out = jnp.einsum('teh,te->th', out_e, cw)
            return out.reshape(b, s, h)
        return _moe_forward(hidden_states, Wg, bg, Wgu, bgu, Wd, bd)

    def _L1_attn_ref(x, w_down_q, w_down_kv, w_up_q, w_up_k, w_up_v, w_out, ln_scale, ln_bias):
        import jax, jax.numpy as jnp
        import numpy as np
        B, S, D = (2, 512, 256)
        H, DH = (16, 64)
        DQL, DKVL = (128, 128)
        DR = 64
        TOPK = 64
        LN_EPS = 1e-05
        ROPE_BASE = 10000.0

        def _rope_tables(seq_len, dim):
            inv_freq = 1.0 / ROPE_BASE ** (np.arange(0, dim, 2, dtype=np.float32) / dim)
            t = np.arange(seq_len, dtype=np.float32)
            freqs = np.outer(t, inv_freq)
            cos = np.concatenate([np.cos(freqs), np.cos(freqs)], -1)[:, ::2]
            sin = np.concatenate([np.sin(freqs), np.sin(freqs)], -1)[:, ::2]
            return (jnp.asarray(cos), jnp.asarray(sin))

        def _apply_rope_subspace(x, d_rope):
            s = x.shape[-2]
            cos, sin = _rope_tables(s, d_rope)
            xr, xp = (x[..., :d_rope], x[..., d_rope:])
            e, o = (xr[..., 0::2], xr[..., 1::2])
            rot = jnp.stack([e * cos - o * sin, e * sin + o * cos], axis=-1).reshape(xr.shape)
            return jnp.concatenate([rot, xp], axis=-1)

        def _reference_tuple_inner(x, w_down_q, w_down_kv, w_up_q, w_up_k, w_up_v, w_out, ln_scale, ln_bias):
            b, s, d = x.shape
            residual = x
            mu = jnp.mean(x, axis=-1, keepdims=True)
            var = jnp.mean((x - mu) ** 2, axis=-1, keepdims=True)
            h = (x - mu) * jax.lax.rsqrt(var + LN_EPS) * ln_scale + ln_bias
            c_q = h @ w_down_q.T
            c_kv = h @ w_down_kv.T
            q = (c_q @ w_up_q.T).reshape(b, s, H, DH).transpose(0, 2, 1, 3)
            k = (c_kv @ w_up_k.T).reshape(b, s, H, DH).transpose(0, 2, 1, 3)
            v = (c_kv @ w_up_v.T).reshape(b, s, H, DH).transpose(0, 2, 1, 3)
            q = _apply_rope_subspace(q, DR)
            k = _apply_rope_subspace(k, DR)
            scale = 1.0 / np.sqrt(DH).astype(np.float32)
            scores = jnp.einsum('bhqd,bhkd->bhqk', q, k) * scale
            _, indices = jax.lax.top_k(scores, min(TOPK, s))
            attn = jax.nn.softmax(scores, axis=-1)
            out = jnp.einsum('bhqk,bhkd->bhqd', attn, v)
            out = out.transpose(0, 2, 1, 3).reshape(b, s, H * DH)
            out = out @ w_out.T + residual
            return (out, indices.astype(jnp.int64))
        return _reference_tuple_inner(x, w_down_q, w_down_kv, w_up_q, w_up_k, w_up_v, w_out, ln_scale, ln_bias)[0]

    def _L1_ffn_ref(hidden_states, gate_w, w_gate, w_up, w_down):
        import jax, jax.numpy as jnp
        import numpy as np
        NUM_EXPERTS = 64
        TOP_K = 8
        HIDDEN = 256
        INTER = 192
        BATCH, SEQ = (1, 256)
        CAPACITY = 64

        def _moe_forward(hidden_states, gate_w, w_gate, w_up, w_down):
            B, S, H = hidden_states.shape
            x = hidden_states.reshape(-1, H)
            T = x.shape[0]
            logits = (x @ gate_w.T).astype(jnp.float32)
            probs = jax.nn.softmax(logits, axis=-1)
            topk_p, topk_i = jax.lax.top_k(probs, TOP_K)
            topk_p = topk_p / jnp.sum(topk_p, axis=-1, keepdims=True)
            flat_e = topk_i.reshape(-1)
            onehot = jax.nn.one_hot(flat_e, NUM_EXPERTS, dtype=jnp.int32)
            pos_all = jnp.cumsum(onehot, axis=0) - 1
            pos = jnp.take_along_axis(pos_all, flat_e[:, None], axis=1)[:, 0]
            x_rep = jnp.repeat(x, TOP_K, axis=0)
            dispatch = jnp.zeros((NUM_EXPERTS, CAPACITY, H), x.dtype)
            dispatch = dispatch.at[flat_e, pos].set(x_rep, mode='drop')
            g = jax.nn.silu(jnp.einsum('ech,eih->eci', dispatch, w_gate))
            u = jnp.einsum('ech,eih->eci', dispatch, w_up)
            y = jnp.einsum('eci,ehi->ech', g * u, w_down)
            valid = pos < CAPACITY
            y_tok = y[flat_e, jnp.minimum(pos, CAPACITY - 1)]
            w = (topk_p.reshape(-1) * valid.astype(topk_p.dtype)).astype(x.dtype)
            out = (y_tok * w[:, None]).reshape(T, TOP_K, H).sum(axis=1)
            return out.reshape(B, S, H)
        return _moe_forward(hidden_states, gate_w, w_gate, w_up, w_down)
    x = L0_attn_X
    x = x + _L0_attn_ref(_layernorm(x, axis=-1), L0_attn_Wq, L0_attn_Wv, L0_attn_q_norm_w, L0_attn_v_norm_w)
    x = x + _L0_ffn_ref(_layernorm(x, axis=-1), L0_ffn_Wg, L0_ffn_bg, L0_ffn_Wgu, L0_ffn_bgu, L0_ffn_Wd, L0_ffn_bd)
    x = x + _L1_attn_ref(_layernorm(x, axis=-1), L1_attn_w_down_q, L1_attn_w_down_kv, L1_attn_w_up_q, L1_attn_w_up_k, L1_attn_w_up_v, L1_attn_w_out, L1_attn_ln_scale, L1_attn_ln_bias)
    x = x + _L1_ffn_ref(_layernorm(x, axis=-1), L1_ffn_gate_w, L1_ffn_w_gate, L1_ffn_w_up, L1_ffn_w_down)
    return x

_drawn_inputs = setup_inputs


def setup_inputs(seed=0):
    import zlib

    import numpy as np

    out = dict(_drawn_inputs(seed))
    spreads = {'L0_attn_q_norm_w': (1.0, 0.2),
     'L0_attn_v_norm_w': (1.0, 0.2),
     'L1_attn_ln_scale': (1.0, 0.6),
     'L1_attn_ln_bias': (0.0, 0.8)}
    factors = {'L0_ffn_Wg': 8.0,
     'L0_ffn_bg': 25.828,
     'L0_ffn_Wgu': 8.0,
     'L0_ffn_bgu': 45.897,
     'L0_ffn_Wd': 8.0,
     'L0_ffn_bd': 64.0,
     'L1_attn_w_down_q': 8.0,
     'L1_attn_w_down_kv': 8.0,
     'L1_attn_w_up_q': 8.0,
     'L1_attn_w_up_k': 8.0,
     'L1_attn_w_up_v': 8.0,
     'L1_attn_w_out': 8.0,
     'L1_ffn_gate_w': 64.0,
     'L1_ffn_w_gate': 64.0,
     'L1_ffn_w_up': 64.0,
     'L1_ffn_w_down': 64.0}
    for name, (base, spread) in spreads.items():
        noise = np.random.default_rng([zlib.crc32(name.encode()), seed]).standard_normal(out[name].shape)
        drawn = base * np.exp(spread * noise) if base else spread * noise
        out[name] = jnp.asarray(drawn.astype(out[name].dtype))
    for name, factor in factors.items():
        out[name] = (out[name] * factor).astype(out[name].dtype)
    return out
```

```python
import numpy as np
import concourse.bass as bass
from concourse import mybir
from contextlib import ExitStack

F32 = mybir.dt.float32
F32R = mybir.dt.float32r
BF16 = mybir.dt.bfloat16
U32 = mybir.dt.uint32
ACT = mybir.ActivationFunctionType
ALU = mybir.AluOpType
X = mybir.AxisListType.X

B, L, D = 2, 2048, 256
T = B * L
P = 128
NT = T // P
TB = L // P
DC = D // P
H0, D0 = 16, 16
H, DH = 16, 64
PAIRS = B * H // 2
QB = 512
NQB = L // QB
KC = L // P
E0, K0, F0 = 16, 2, 256
E1, K1_, F1 = 64, 8, 192
CAP = 64
ST0 = T * K0 // P + E0 - 1
BLOCKS0 = E0 * NT + 1
LN_EPS = 1e-5
RMS_EPS = 1e-8
DROP = 1 << 20
HALF = DH // 2

CONST = [("ident", P), ("causal", P), ("before", P), ("blocks", P), ("parity", 2), ("keep", NT),
         ("iota", E1), ("token", NT), ("tiles", ST0 + 1)]


def const_at(name):
    at = 0
    for n, w in CONST:
        if n == name:
            return at, at + w
        at += w
    raise KeyError(name)


def shape_constants():
    c = np.zeros((P, sum(w for _, w in CONST)), np.float32)
    r = np.arange(P)

    def put(name, value):
        a, b = const_at(name)
        c[:, a:b] = value
    put("ident", np.eye(P))
    put("causal", r[:, None] <= r[None, :])
    put("before", r[:, None] < r[None, :])
    put("blocks", r[:, None] // D0 == r[None, :] // D0)
    put("parity", np.stack([(r // D0) % 2 == 0, (r // D0) % 2 == 1], 1))
    put("keep", (np.arange(NT) % TB != TB - 1)[None, :])
    put("iota", np.arange(E1)[None, :])
    put("token", (np.arange(NT)[None, :] * P + r[:, None]))
    put("tiles", np.arange(ST0 + 1)[None, :])
    return c


def rope_constants():
    inv = 1.0 / 10000.0 ** (np.arange(0, DH, 2, dtype=np.float32) / DH)
    f = np.outer(np.arange(L, dtype=np.float32), inv)
    cos = np.concatenate([np.cos(f), np.cos(f)], -1)[:, ::2]
    sin = np.concatenate([np.sin(f), np.sin(f)], -1)[:, ::2]
    t = np.stack([np.concatenate([cos, cos], 1), np.concatenate([-sin, sin], 1)], 1)
    return np.ascontiguousarray(t.reshape(TB, P, 2 * DH).transpose(1, 0, 2)).astype(np.float32)


class Chain:

    def __init__(self, eng, sem):
        self.eng, self.sem, self.base, self.n = eng, sem, 0, 0

    def __call__(self, ins):
        self.n += 1
        ins.then_inc(self.sem, 1)
        self.eng.wait_ge(self.sem, self.base + self.n)

    def begin(self, base):
        self.base, self.n = base, 0


def pipeline(eng, n, unroll, prologue, step, peel_first=False):
    prologue()
    if peel_first:
        for r in range(unroll):
            step(r, r)
    with eng.Fori(unroll if peel_first else 0, n - 2 * unroll + 1, unroll) as j:
        for r in range(unroll):
            step(j + r, r)
    for r in range(unroll):
        step(n - unroll + r, r)


def exists(i, n):
    return not isinstance(i, int) or i < n


def nothing():
    pass


def stand_alone(eng, turns):
    eng.sem_inc(turns, 1)


class Kernel:
    def __init__(self, nc, ins, out):
        self.nc, self.ins, self.out = nc, ins, out
        self.sems = 0

    def build(self):
        nc = self.nc
        self.x_acc = nc.dram_tensor("x_acc", (T, D), F32)
        self.x_odd = nc.dram_tensor("x_odd", (T, D), F32)
        self.out_odd = nc.dram_tensor("out_odd", (T, D), F32)
        self.xn_dram = nc.dram_tensor("xn_dram", (T, D), F32)
        self.table0 = nc.dram_tensor("table0", (BLOCKS0 * P, 2), F32)
        self.table1 = nc.dram_tensor("table1", (E1 * CAP, 2), F32)
        self.qkv = nc.dram_tensor("qkv", (PAIRS, L, 3, P), F32)
        self.o_dram = nc.dram_tensor("o_dram", (PAIRS, P, L), F32)
        self.counts_sb = None
        with ExitStack() as keep:
            self.C = keep.enter_context(nc.sbuf_tensor("C", [P, sum(w for _, w in CONST)], F32))
            self.tri = keep.enter_context(nc.sbuf_tensor("tri", [P, P], BF16))
            self.ones_bf = keep.enter_context(nc.sbuf_tensor("ones_bf", [P, P], BF16))
            self.eps = keep.enter_context(nc.sbuf_tensor("eps", [P, 2], F32))
            with ExitStack() as xs:
                self.x = xs.enter_context(nc.sbuf_tensor("x_sb", [P, NT, D], F32))
                self.linear_attention()
                with ExitStack() as moe0:
                    self.tile_expert = moe0.enter_context(nc.sbuf_tensor("tile_expert", [1, 2, ST0 + 1], U32))
                    self.wgu0 = moe0.enter_context(nc.sbuf_tensor("wgu0", [P, E0, DC, 2 * F0], F32))
                    self.wd0 = moe0.enter_context(nc.sbuf_tensor("wd0", [P, E0, DC, D], F32))
                    self.bias0 = moe0.enter_context(nc.sbuf_tensor("bias0", [3, E0, 2 * F0 + D], BF16))
                    self.route(0, E0, K0, self.table0, self.x_acc[:])
                    self.experts(0)
            self.project()
            self.softmax_attention()
            with ExitStack() as xs:
                self.x = xs.enter_context(nc.sbuf_tensor("x_sb2", [P, NT, D], F32))
                self.output_projection()
                self.route(1, E1, K1_, self.table1, self.out)
            self.experts(1)
            self.add_odd()

    def const(self, name):
        a, b = const_at(name)
        return self.C[:, a:b]

    def scope(self, stage):
        ctx, nc = ExitStack(), self.nc
        sb = lambda name, shape, dt=F32: ctx.enter_context(nc.sbuf_tensor(f"{stage}_{name}", shape, dt))
        ps = lambda name, shape, dt=F32: ctx.enter_context(nc.psum_tensor(f"{stage}_{name}", shape, dt))
        held = []

        def sem(name):
            held.append(nc.alloc_semaphore(f"{stage}_{name}"))
            return held[-1]

        def release():
            nc.clear_and_free_semaphores(held)
            nc.all_engine_barrier()
        ctx.callback(release)
        return ctx, sb, ps, sem

    def linear_attention(self):
        nc, ins, x = self.nc, self.ins, self.x
        ctx, sb, ps, sem = self.scope("la")
        with ctx:
            wqv = sb("wqv", [P, DC, 2 * D])
            normw = sb("normw", [P, 2 * D])
            stats = sb("stats", [P, 6])
            mv = sb("mv", [P, NT, 2])
            agg = sb("agg", [P, 2])
            std = sb("std", [P, NT])
            rstd = sb("rstd", [P, NT])
            xn = sb("xn", [P, 4, D])
            xnT = sb("xnT", [P, 4, D])
            sq = sb("sq", [P, 2 * D])
            ss = sb("ss", [P, 2 * H0])
            rt = sb("rt", [P, 2 * H0])
            rr = sb("rr", [P, 2 * H0])
            qv1 = sb("qv1", [P, 2 * D])
            qv = sb("qv", [P, 4, 2 * D])
            qz = sb("qz", [P, 2, DC, 2, P])
            qf = sb("qf", [P, 2, DC, P])
            at = sb("at", [P, H0, P])
            state = sb("state", [P, DC, P])
            kvm = sb("kvm", [P, DC, P])
            fill = sb("fill", [P, BLOCKS0, 2])
            zero = sb("zero", [P, 4, D])
            ps_t = ps("ps_t", [P, 512])
            ps_qv = ps("ps_qv", [P, 512])
            ps_qT = ps("ps_qT", [P, 512])
            ps_a = ps("ps_a", [P, 4, 512])
            ps_o = ps("ps_o", [P, 512])
            names = ("turns mv_ready consts x weights const_ready fill_ready zero_ready filled own_dve kv_masked std_ready "
                     "xn_ready t_ready xnT_ready "
                     "qvps_ready sq_ready ss_ready rt_ready qv_ready qT_ready qz_ready a_ready at_ready "
                     "o_done state_ready xs_done").split()
            s = {n: sem(n) for n in names}
            ident, causal = self.const("ident"), self.const("causal")
            blocks, parity, keep = self.const("blocks"), self.const("parity"), self.const("keep")
            block = ctx.enter_context(nc.Block())

            @block.sync
            def _(sp):
                sp.dma_start(self.C[:], ins["consts"]).then_inc(s["consts"], 16)
                sp.dma_start(x[:], ins["X"].rearrange("(n p) d -> p n d", p=P)).then_inc(s["x"], 16)
                for w, name in enumerate(("WqT", "WvT")):
                    sp.dma_start(wqv[:, :, w * D:(w + 1) * D],
                                 ins[name].rearrange("(c p) n -> p c n", p=P)).then_inc(s["weights"], 16)
                for w, name in enumerate(("qw", "vw")):
                    sp.dma_start(normw[:, w * D:(w + 1) * D],
                                 ins[name].partition_broadcast(P)).then_inc(s["weights"], 16)
                sp.wait_ge(s["fill_ready"], 2)
                sp.dma_start(self.table0[:].rearrange("(n p) w -> p n w", p=P), fill[:]).then_inc(s["filled"], 16)
                sp.dma_start(self.table1[:].rearrange("(n p) w -> p n w", p=P), fill[:, 0:E1 * CAP // P])\
                    .then_inc(s["filled"], 16)
                sp.wait_ge(s["zero_ready"], 1)
                for acc in (self.x_odd, self.out_odd):
                    for n in range(0, NT, 4):
                        sp.dma_start(acc[:].rearrange("(n p) d -> p n d", p=P)[:, n:n + 4], zero[:]).then_inc(s["filled"], 16)
                sp.wait_ge(s["filled"], 32 + 16 * 2 * NT // 4)

            @block.gpsimd
            def _(pool):
                pool.memset(self.eps[:, 0:1], LN_EPS).then_inc(s["const_ready"], 1)
                pool.memset(self.eps[:, 1:2], RMS_EPS).then_inc(s["const_ready"], 1)
                pool.memset(self.ones_bf[:], 1.0)
                pool.memset(fill[:].bitcast(U32)[:, :, 0], DROP).then_inc(s["fill_ready"], 1)
                pool.memset(fill[:, :, 1], 0.0).then_inc(s["fill_ready"], 1)
                pool.memset(zero[:], 0.0).then_inc(s["zero_ready"], 1)

            @block.vector
            def _(dve):
                link = Chain(dve, s["own_dve"])
                dve.memset(state[:], 0.0).then_inc(s["state_ready"], 1)
                dve.wait_ge(s["consts"], 16)
                dve.tensor_copy(self.tri[:], self.const("before"))
                dve.wait_ge(s["x"], 16)
                self.statistics(dve, link, s, x, stats, agg, mv)
                dve.wait_ge(s["std_ready"], 1)
                link.begin(2 * NT)
                link(dve.reciprocal(rstd[:], std[:]))

                def tokens(i, r):
                    dve.tensor_scalar(xn[:, r % 4], x[:, bass.ds(i, 1), :].squeeze(1),
                                      mv[:, bass.ds(i, 1), 0], rstd[:, bass.ds(i, 1)],
                                      ALU.subtract, ALU.mult).then_inc(s["xn_ready"], 1)
                dve.wait_ge(s["weights"], 64)
                done = 2 * NT + 1

                def normalise(i, r):
                    link.begin(i * 2 + done)
                    dve.wait_ge(s["sq_ready"], i + 1)
                    dve.tensor_reduce(ss[:], sq[:].rearrange("p (h d) -> p h d", d=D0), X, ALU.add)\
                        .then_inc(s["ss_ready"], 1)
                    dve.wait_ge(s["rt_ready"], i + 1)
                    link(dve.reciprocal(rr[:], rt[:]))
                    link(dve.tensor_tensor(qv1[:].rearrange("p (h d) -> p h d", d=D0),
                                           ps_qv[:].rearrange("p (h d) -> p h d", d=D0),
                                           rr[:].unsqueeze(2).broadcast_to([P, 2 * H0, D0]), ALU.mult))
                    dve.tensor_tensor(qv[:, r % 4], qv1[:], normw[:], ALU.mult).then_inc(s["qv_ready"], 1)

                def step(i, r):
                    atv = at[:].rearrange("p (c j r) l -> p j c r l", c=DC, j=4)
                    for j in range(4):
                        dve.wait_ge(s["a_ready"], i * 4 + (j + 1))
                        m = dve.tensor_tensor(atv[:, j], ps_a[:, j].rearrange("p (c r l) -> p c r l", c=DC, r=2),
                                              causal.unsqueeze(1).unsqueeze(1).broadcast_to([P, DC, 2, P]), ALU.mult)
                    m.then_inc(s["at_ready"], 1)
                    if exists(i + 2, NT):
                        normalise(i + 2, r + 2)
                    dve.wait_ge(s["o_done"], i + 1)
                    dve.scalar_tensor_tensor(kvm[:], ps_o[:, D:2 * D].rearrange("p (c e) -> p c e", c=DC),
                                             keep[:, bass.ds(i, 1)], blocks.unsqueeze(1).broadcast_to([P, DC, P]),
                                             ALU.mult, ALU.mult).then_inc(s["kv_masked"], 1)
                    dve.tensor_tensor(x[:, bass.ds(i, 1), :].squeeze(1), ps_o[:, 0:D],
                                      x[:, bass.ds(i, 1), :].squeeze(1), ALU.add)
                    dve.wait_ge(s["kv_masked"], i + 1)
                    dve.scalar_tensor_tensor(state[:], state[:], keep[:, bass.ds(i, 1)], kvm[:],
                                             ALU.mult, ALU.add).then_inc(s["state_ready"], 1)
                    if exists(i + 4, NT):
                        tokens(i + 4, r)

                def prologue():
                    for i in range(4):
                        tokens(i, i)
                    normalise(0, 0)
                    normalise(1, 1)
                pipeline(dve, NT, 4, prologue, step)

            @block.scalar
            def _(act):
                act.wait_ge(s["const_ready"], 2)
                act.wait_ge(s["mv_ready"], NT)
                act.activation(std[:], mv[:, :, 1], ACT.Sqrt, bias=self.eps[:, 0:1]).then_inc(s["std_ready"], 1)

                def keys(i, r):
                    act.wait_ge(s["t_ready"], i + 1)
                    act.activation(xnT[:, r % 4], ps_t[:, 0:D], ACT.Copy).then_inc(s["xnT_ready"], 1)

                def squares(i):
                    act.wait_ge(s["qvps_ready"], i + 1)
                    act.activation(sq[:], ps_qv[:], ACT.Square).then_inc(s["sq_ready"], 1)

                def roots(i):
                    act.wait_ge(s["ss_ready"], i + 1)
                    act.activation(rt[:], ss[:], ACT.Sqrt, bias=self.eps[:, 1:2], scale=1.0 / D0)\
                        .then_inc(s["rt_ready"], 1)

                def queries(i, r):
                    act.wait_ge(s["qT_ready"], i + 1)
                    src = ps_qT[:, 0:D].rearrange("p (c l) -> p c l", c=DC)
                    act.activation(qz[:, r % 2, :, 0, :], src, ACT.Copy, scale=parity[:, 0:1])
                    act.activation(qz[:, r % 2, :, 1, :], src, ACT.Copy, scale=parity[:, 1:2])
                    act.activation(qf[:, r % 2], src, ACT.Copy).then_inc(s["qz_ready"], 1)

                def prologue():
                    for i in range(3):
                        keys(i, i)
                    for i in range(2):
                        squares(i)
                        roots(i)
                    queries(0, 0)

                def step(i, r):
                    if exists(i + 3, NT):
                        keys(i + 3, r + 3)
                    if exists(i + 2, NT):
                        squares(i + 2)
                    if exists(i + 1, NT):
                        queries(i + 1, r + 1)
                    if exists(i + 2, NT):
                        roots(i + 2)
                pipeline(act, NT, 4, prologue, step)

            @block.tensor
            def _(pe):
                pe.wait_ge(s["consts"], 16)
                pe.wait_ge(s["weights"], 64)

                def keys(i, r):
                    pe.wait_ge(s["xn_ready"], i + 1)
                    if not isinstance(i, int) or i > 0:
                        pe.wait_ge(s["xnT_ready"], i)
                    for c in range(DC):
                        m = pe.transpose(ps_t[:, c * P:(c + 1) * P], xn[:, r % 4, c * P:(c + 1) * P], ident)
                    m.then_inc(s["t_ready"], 1)

                def project(i, r):
                    pe.wait_ge(s["xnT_ready"], i + 1)
                    if not isinstance(i, int) or i > 0:
                        pe.wait_ge(s["qv_ready"], i)
                    for c in range(DC):
                        m = pe.matmul(ps_qv[:], xnT[:, r % 4, c * P:(c + 1) * P], wqv[:, c],
                                      start=c == 0, stop=c == DC - 1)
                    m.then_inc(s["qvps_ready"], 1)

                def queries(i, r):
                    pe.wait_ge(s["qv_ready"], i + 1)
                    for c in range(DC):
                        m = pe.transpose(ps_qT[:, c * P:(c + 1) * P], qv[:, r % 4, c * P:(c + 1) * P], ident)
                    m.then_inc(s["qT_ready"], 1)

                def step(i, r):
                    pe.wait_ge(s["qz_ready"], i + 1)
                    for j in range(4):
                        f = slice(32 * j, 32 * j + 32)
                        for c in range(DC):
                            m = pe.matmul(ps_a[:, j, c * D:(c + 1) * D], xnT[f, r, c * P:(c + 1) * P],
                                          qz[f, r % 2, c].rearrange("p r l -> p (r l)"), start=True, stop=True)
                        m.then_inc(s["a_ready"], 1)
                    if exists(i + 3, NT):
                        keys(i + 3, r + 3)
                    if exists(i + 2, NT):
                        project(i + 2, r + 2)
                    if exists(i + 1, NT):
                        queries(i + 1, r + 1)
                    pe.wait_ge(s["state_ready"], i + 1)
                    for c in range(DC):
                        pe.matmul(ps_o[:, D + c * P:D + (c + 1) * P], xn[:, r, c * P:(c + 1) * P],
                                  qv[:, r, D + c * P:D + (c + 1) * P], start=True, stop=True, skip_group_check=True)
                    for c in range(DC):
                        pe.matmul(ps_o[:, c * P:(c + 1) * P], qf[:, r % 2, c], state[:, c], start=c == 0, stop=False,
                                  skip_group_check=True)
                    pe.wait_ge(s["at_ready"], i + 1)
                    for h in range(H0):
                        m = pe.matmul(ps_o[:, h * D0:(h + 1) * D0], at[:, h, :], qv[:, r, D + h * D0:D + (h + 1) * D0],
                                      start=False, stop=h == H0 - 1, skip_group_check=True)
                    m.then_inc(s["o_done"], 1)

                def prologue():
                    for i in range(3):
                        keys(i, i)
                    for i in range(2):
                        project(i, i)
                    queries(0, 0)
                pipeline(pe, NT, 4, prologue, step)

    def statistics(self, dve, link, s, x, stats, agg, mv, first=0, end=NT):
        with dve.Fori(first, end) as i:
            link.begin(i * 2)
            link(dve.bn_stats(stats[:], x[:, bass.ds(i, 1), :].squeeze(1)))
            stand_alone(dve, s["turns"])
            link(dve.bn_aggr(agg[:], stats[:]))
            dve.tensor_copy(mv[:, bass.ds(i, 1), :].squeeze(1), agg[:]).then_inc(s["mv_ready"], 1)

    def route(self, moe, E, K, table, residual):
        nc, ins, x = self.nc, self.ins, self.x
        ctx, sb, ps, sem = self.scope(f"rt{moe}")
        SPAN = T if moe == 0 else CAP
        ROWS = BLOCKS0 * P if moe == 0 else E1 * CAP
        with ctx:
            stats = sb("stats", [P, 6])
            mv = sb("mv", [P, NT, 2])
            agg = sb("agg", [P, 2])
            std = sb("std", [P, NT])
            rstd = sb("rstd", [P, NT])
            xn = sb("xn", [P, 4, D])
            xnT = sb("xnT", [P, 2, D])
            wg = sb("wg", [P, DC, E])
            bg = sb("bg", [P, E])
            lg = sb("lg", [P, E])
            pr = sb("pr", [P, E])
            small = sb("small", [P, 4])
            top = sb("top", [P, 8])
            topi = sb("topi", [P, 8], U32)
            idx = sb("idx", [P, K])
            pos = sb("pos", [P, K])
            hot = sb("hot", [P, K, E])
            hotp = sb("hotp", [P, K, E])
            mask = sb("mask", [P, 2, E], BF16)
            seen = sb("seen", [P, E], BF16)
            slotf = sb("slotf", [P, K])
            over = sb("over", [P, K])
            wsum = sb("wsum", [P, 2])
            slot = sb("slot", [P, 4, K], U32)
            entry = sb("entry", [P, 4, K, 2])
            ps_t = ps("ps_t", [P, 512])
            ps_l = ps("ps_l", [P, 512])
            ps_p = ps("ps_p", [P, 512])
            if moe == 0:
                cnt, ntl, endt, off, onesf = (sb(n, [P, E]) for n in ("cnt", "ntl", "endt", "off", "onesf"))
                cnti = sb("cnti", [P, E], U32)
                below = sb("below", [1, ST0 + 1, E0])
                begin = sb("begin", [1, ST0 + 1, E0])
                texp, tbeg, live, blk = (sb(n, [1, ST0 + 1]) for n in ("texp", "tbeg", "live", "blk"))
                bsrc = sb("bsrc", [E0, 2 * F0 + D])
                brest = sb("brest", [E0, 2 * F0 + D])
                bpart = sb("bpart", [E0, 3, 2 * F0 + D], BF16)
            names = ("turns mv_ready weights own std_ready xn_ready xn0_out xn1_out xn2_out xn3_out x_out t_ready "
                     "xnT_ready l_ready e_ready e_go mask_ready pos_ready cnt_ready w_go w_ready staged "
                     "scat0 scat1 scat2 scat3 experts_in bias_in bias_split bias_out").split()
            s = {n: sem(n) for n in names}
            ident, iota = self.const("ident"), self.const("iota")[:, 0:E]
            block = ctx.enter_context(nc.Block())
            PER = 10 if moe == 0 else 17
            STATS = 2 * NT + 1

            @block.sync
            def _(sp):
                sp.dma_start(wg[:], ins[f"router{moe}"].rearrange("(c p) n -> p c n", p=P)).then_inc(s["weights"], 16)
                if moe == 0:
                    sp.dma_start(bg[:], ins["bg"].partition_broadcast(P)).then_inc(s["weights"], 16)
                    sp.dma_start(bsrc[:, 0:2 * F0], ins["bgu"]).then_inc(s["bias_in"], 16)
                    sp.dma_start(bsrc[:, 2 * F0:], ins["bd"]).then_inc(s["bias_in"], 16)
                sp.dma_start(residual.rearrange("(n p) d -> p n d", p=P), x[:]).then_inc(s["x_out"], 16)
                if moe == 0:
                    for e in range(E0):
                        sp.dma_start(self.wgu0[:, e], ins["Wgu"][e].rearrange("(c p) n -> p c n", p=P))                            .then_inc(s["experts_in"], 16)
                        sp.dma_start(self.wd0[:, e], ins["Wd"][e].rearrange("(c p) n -> p c n", p=P))                            .then_inc(s["experts_in"], 16)
                rows = self.xn_dram[:].rearrange("(n p) d -> p n d", p=P)
                with sp.Fori(0, NT - 3, 4) as i:
                    for r in range(4):
                        sp.wait_ge(s["xn_ready"], i + (r + 1))
                        sp.dma_start(rows[:, bass.ds(i + r, 1), :].squeeze(1), xn[:, r]).then_inc(s[f"xn{r}_out"], 16)
                if moe == 0:
                    sp.wait_ge(s["bias_split"], 5)
                    for e in range(E0):
                        for k in range(3):
                            sp.dma_start(self.bias0[k:k + 1, e], bpart[e:e + 1, k]).then_inc(s["bias_out"], 16)
                    sp.wait_ge(s["bias_out"], 48 * E0)
                    sp.wait_ge(s["experts_in"], 32 * E0)
                sp.wait_ge(s["x_out"], 16)
                for r in range(4):
                    sp.wait_ge(s[f"xn{r}_out"], 4 * NT + 16)

            @block.vector
            def _(dve):
                link = Chain(dve, s["own"])
                self.statistics(dve, link, s, x, stats, agg, mv)
                dve.wait_ge(s["std_ready"], 1)
                link.begin(2 * NT)
                link(dve.reciprocal(rstd[:], std[:]))
                dve.wait_ge(s["weights"], 32 if moe == 0 else 16)
                dve.memset(seen[:], 0.0)
                if moe == 0:
                    dve.wait_ge(s["bias_in"], 32)
                    part = Chain(dve, s["bias_split"])
                    part(dve.tensor_copy(bpart[:, 0], bsrc[:]))
                    part(dve.tensor_tensor(brest[:], bsrc[:], bpart[:, 0], ALU.subtract))
                    part(dve.tensor_copy(bpart[:, 1], brest[:]))
                    part(dve.tensor_tensor(bsrc[:], brest[:], bpart[:, 1], ALU.subtract))
                    part(dve.tensor_copy(bpart[:, 2], bsrc[:]))

                def tokens(i, r):
                    dve.wait_ge(s[f"xn{r % 4}_out"], i * 4 + (16 - 4 * (r % 4)))
                    dve.tensor_scalar(xn[:, r % 4], x[:, bass.ds(i, 1), :].squeeze(1), mv[:, bass.ds(i, 1), 0],
                                      rstd[:, bass.ds(i, 1)], ALU.subtract, ALU.mult).then_inc(s["xn_ready"], 1)

                def step(i, r):
                    link.begin(i * PER + STATS)
                    if exists(i + 2, NT):
                        tokens(i + 2, r + 2)
                    dve.wait_ge(s["l_ready"], i + 1)
                    if moe == 0:
                        link(dve.tensor_tensor(lg[:], ps_l[:, 0:E], bg[:], ALU.add))
                        scores = lg
                    else:
                        link(dve.tensor_reduce(small[:, 0:1], ps_l[:, 0:E], X, ALU.max))
                        dve.tensor_scalar(small[:, 1:2], small[:, 0:1], -1.0, None, ALU.mult).then_inc(s["e_go"], 1)
                        dve.wait_ge(s["e_ready"], i + 1)
                        link(dve.tensor_reduce(small[:, 2:3], lg[:], X, ALU.add))
                        link(dve.reciprocal(small[:, 3:4], small[:, 2:3]))
                        link(dve.tensor_scalar(pr[:], lg[:], small[:, 3:4], None, ALU.mult))
                        scores = pr
                    stand_alone(dve, s["turns"])
                    link(dve.max(top[:], scores[:]))
                    if moe == 0:
                        if not isinstance(i, int) or i > 0:
                            dve.wait_ge(s["w_ready"], i)
                        dve.tensor_tensor(over[:, 0:1], top[:, 0:1], top[:, 1:2], ALU.subtract)
                        dve.tensor_tensor(over[:, 1:2], top[:, 1:2], top[:, 0:1], ALU.subtract).then_inc(s["w_go"], 1)
                    stand_alone(dve, s["turns"])
                    link(dve.max_index(topi[:], top[:], scores[:]))
                    link(dve.tensor_copy(idx[:], topi[:, 0:K]))
                    link(dve.tensor_tensor(hot[:], iota.unsqueeze(1).broadcast_to([P, K, E]),
                                           idx[:].unsqueeze(2).broadcast_to([P, K, E]), ALU.is_equal))
                    with nc.allow_low_precision(reason="sums of one-hot rows: 0 or 1"):
                        link(dve.tensor_reduce(mask[:, r % 2], hot[:].rearrange("p k e -> p e k"), X, ALU.add))
                    dve.sem_inc(s["mask_ready"], 1)
                    dve.wait_ge(s["pos_ready"], i + 1)
                    link(dve.tensor_tensor(seen[:], seen[:], mask[:, r % 2], ALU.add))
                    link(dve.tensor_tensor(hotp[:], hot[:],
                                           ps_p[:, 0:E].unsqueeze(1).broadcast_to([P, K, E]), ALU.mult))
                    link(dve.tensor_reduce(pos[:], hotp[:], X, ALU.add))
                    link(dve.scalar_tensor_tensor(slotf[:], idx[:], float(SPAN), pos[:], ALU.mult, ALU.add))
                    if moe == 1:
                        link(dve.tensor_scalar(over[:], pos[:], float(CAP), float(DROP), ALU.is_ge, ALU.mult))
                        link(dve.tensor_tensor(slotf[:], slotf[:], over[:], ALU.add))
                        link(dve.tensor_reduce(wsum[:, 0:1], top[:, 0:K], X, ALU.add))
                        link(dve.reciprocal(wsum[:, 1:2], wsum[:, 0:1]))
                    if not isinstance(i, int) or i >= 4:
                        dve.wait_ge(s[f"scat{r}"], i * (4 * K) - 4 * K * r)
                        stand_alone(dve, s["turns"])
                    dve.tensor_copy(slot[:, r], slotf[:])
                    if moe == 1:
                        dve.tensor_scalar(entry[:, r, :, 1], top[:, 0:K], wsum[:, 1:2], None, ALU.mult)
                    dve.tensor_copy(entry[:, r].bitcast(U32)[:, :, 0],
                                    self.const("token")[:, bass.ds(i, 1)].broadcast_to([P, K])).then_inc(s["staged"], 1)
                    dve.wait_ge(s["staged"], i + 1)
                    assert link.n == PER, link.n

                def prologue():
                    tokens(0, 0)
                    tokens(1, 1)
                pipeline(dve, NT, 4, prologue, step, peel_first=True)
                if moe == 0:
                    link.begin(STATS + NT * PER)
                    dve.memset(onesf[:], 1.0)
                    dve.wait_ge(s["cnt_ready"], 1)
                    link(dve.tensor_scalar(cnt[:], ps_p[:, 0:E], float(P - 1), None, ALU.add))
                    link(dve.tensor_copy(cnti[:], cnt[:]))
                    link(dve.tensor_scalar(cnti[:], cnti[:], 7, None, ALU.logical_shift_right))
                    link(dve.tensor_copy(ntl[:], cnti[:]))
                    link(dve.tensor_tensor_scan(endt[:], onesf[:], ntl[:], 0.0, ALU.mult, ALU.add))
                    link(dve.tensor_tensor(off[:], endt[:], ntl[:], ALU.subtract))
                    every = [1, ST0 + 1, E]
                    tiles = self.const("tiles")[0:1]
                    link(dve.tensor_tensor(below[:], endt[0:1, :].unsqueeze(1).broadcast_to(every),
                                           tiles.unsqueeze(2).broadcast_to(every), ALU.is_le))
                    link(dve.tensor_reduce(texp[:], below[:], X, ALU.add))
                    link(dve.tensor_scalar(self.tile_expert[:, 0], texp[:], float(E - 1), None, ALU.min))
                    link(dve.tensor_tensor(begin[:], iota[0:1].unsqueeze(1).broadcast_to(every),
                                           texp[:].unsqueeze(2).broadcast_to(every), ALU.is_equal))
                    link(dve.tensor_tensor(begin[:], begin[:], off[0:1, :].unsqueeze(1).broadcast_to(every), ALU.mult))
                    link(dve.tensor_reduce(tbeg[:], begin[:], X, ALU.add))
                    link(dve.tensor_tensor(tbeg[:], tiles, tbeg[:], ALU.subtract))
                    link(dve.scalar_tensor_tensor(blk[:], texp[:], float(NT), tbeg[:], ALU.mult, ALU.add))
                    link(dve.tensor_scalar(live[:], texp[:], float(E), None, ALU.is_lt))
                    link(dve.tensor_scalar(blk[:], blk[:], float(1 - BLOCKS0), None, ALU.add))
                    link(dve.tensor_tensor(blk[:], blk[:], live[:], ALU.mult))
                    link(dve.tensor_scalar(self.tile_expert[:, 1], blk[:], float(BLOCKS0 - 1), None, ALU.add))

            @block.scalar
            def _(act):
                for r in range(4):
                    act.sem_inc(s[f"xn{r}_out"], 16)
                act.wait_ge(s["mv_ready"], NT)
                act.activation(std[:], mv[:, :, 1], ACT.Sqrt, bias=self.eps[:, 0:1]).then_inc(s["std_ready"], 1)

                def tokens(i, r):
                    act.wait_ge(s["t_ready"], i + 1)
                    act.activation(xnT[:, r % 2], ps_t[:, 0:D], ACT.Copy).then_inc(s["xnT_ready"], 1)

                def step(i, r):
                    if exists(i + 1, NT):
                        tokens(i + 1, r + 1)
                    if moe == 1:
                        act.wait_ge(s["e_go"], i + 1)
                        act.activation(lg[:], ps_l[:, 0:E], ACT.Exp, bias=small[:, 1:2]).then_inc(s["e_ready"], 1)
                    else:
                        act.wait_ge(s["w_go"], i + 1)
                        if not isinstance(i, int) or i >= 4:
                            act.wait_ge(s[f"scat{r}"], i * (4 * K) - 4 * K * r)
                        act.activation(entry[:, r, :, 1], over[:], ACT.Sigmoid).then_inc(s["w_ready"], 1)
                pipeline(act, NT, 4, lambda: tokens(0, 0), step, peel_first=True)

            @block.tensor
            def _(pe):
                pe.wait_ge(s["weights"], 32 if moe == 0 else 16)

                def tokens(i, r):
                    pe.wait_ge(s["xn_ready"], i + 1)
                    for c in range(DC):
                        m = pe.transpose(ps_t[:, c * P:(c + 1) * P], xn[:, r % 4, c * P:(c + 1) * P], ident)
                    m.then_inc(s["t_ready"], 1)

                def logits(i, r):
                    pe.wait_ge(s["xnT_ready"], i + 1)
                    for c in range(DC):
                        m = pe.matmul(ps_l[:, 0:E], xnT[:, r % 2, c * P:(c + 1) * P], wg[:, c], start=c == 0, stop=c == DC - 1)
                    m.then_inc(s["l_ready"], 1)

                def step(i, r):
                    logits(i, r)
                    if exists(i + 1, NT):
                        tokens(i + 1, r + 1)
                    pe.wait_ge(s["mask_ready"], i + 1)
                    pe.matmul(ps_p[:, 0:E], self.tri[:], mask[:, r % 2], start=True, stop=False)
                    pe.matmul(ps_p[:, 0:E], self.ones_bf[:], seen[:], start=False, stop=True).then_inc(s["pos_ready"], 1)
                pipeline(pe, NT, 4, lambda: tokens(0, 0), step)
                if moe == 0:
                    pe.wait_ge(s["own"], STATS + NT * PER)
                    pe.matmul(ps_p[:, 0:E], self.ones_bf[:], seen[:], start=True, stop=True).then_inc(s["cnt_ready"], 1)

            @block.gpsimd
            def _(pool):
                with pool.Fori(0, NT - 3, 4) as i:
                    for r in range(4):
                        pool.wait_ge(s["staged"], i + (r + 1))
                        stand_alone(pool, s["turns"])
                        if moe == 0:
                            pool.wait_ge(s["w_ready"], i + (r + 1))
                            stand_alone(pool, s["turns"])
                        for k in range(K):
                            pool.indirect_dma_start(table[:], bass.IndirectOffsetOnAxis(ap=slot[:, r, k:k + 1], axis=0),
                                                    entry[:, r, k, :], None, bounds_check=ROWS - 1, oob_is_err=False)                                .then_inc(s[f"scat{r}"], 16)
                for r in range(4):
                    pool.wait_ge(s[f"scat{r}"], 4 * K * NT)

    def experts(self, moe):
        nc, ins = self.nc, self.ins
        R, F, N = (P, F0, ST0 + 1) if moe == 0 else (CAP, F1, E1)
        FK = 128 if moe == 0 else 96
        targets = (self.x_acc[:], self.x_odd[:]) if moe == 0 else (self.out, self.out_odd[:])
        RING = 4
        WR = 8
        U = 4 if moe == 0 else WR
        ctx, sb, ps, sem = self.scope(f"ex{moe}")
        with ctx:
            if moe == 0:
                ent = sb("ent", [R, RING, 2])
            else:
                ent = sb("ent", [R, N, 2])
            sid = sb("sid", [R, RING, 1], U32)
            wt = sb("wt", [R, RING])
            xg = sb("xg", [R, RING, D])
            xgT = sb("xgT", [P, 2, DC, R])
            gate = sb("gate", [R, F])
            sig = sb("sig", [R, 2, F])
            glu = sb("glu", [R, F])
            up = sb("up", [R, F])
            hid = sb("hid", [R, 2, F])
            hidT = sb("hidT", [FK, 2, R])
            y = sb("y", [R, 2, D])
            if moe == 1:
                wgu = sb("wgu", [P, WR, DC, 2 * F1])
                wd = sb("wd", [FK, WR, 2, D])
            ps_t = ps("ps_t", [P, 512])
            ps_g = ps("ps_g", [P, 2, 512])
            ps_h = ps("ps_h", [P, 512])
            ps_y = ps("ps_y", [P, 2, 512])
            names = ("turns cleared entries e0 e1 e2 e3 sid_ready g0 g1 g2 g3 t_ready xT_ready g_ready gate_ready "
                     "sig_ready hid_ready h_ready hT_ready y_ready ys_ready scat0 scat1 own w0 w1 w2 w3 w4 w5 w6 w7").split()
            s = {n: sem(n) for n in names}
            ident = self.const("ident")
            block = ctx.enter_context(nc.Block())
            LINKS = 2 if moe == 0 else 1

            @block.sync
            def _(sp):
                if moe == 0:
                    blocks = self.table0[:].rearrange("(n p) w -> p n w", p=P)

                    def entries(i, r):
                        b = sp.value_load(self.tile_expert[0:1, 1, bass.ds(i, 1)], min_val=0, max_val=BLOCKS0 - 1)
                        sp.dma_start(ent[:, r % RING], blocks[:, bass.ds(b, 1)].squeeze(1)).then_inc(s[f"e{r % RING}"], 16)

                    for i in range(RING):
                        entries(i, i)
                    with sp.Fori(0, N - 2 * RING + 1, RING) as j:
                        for r in range(RING):
                            sp.wait_ge(s["sid_ready"], j + (r + 1))
                            entries(j + (r + RING), r)
                else:
                    sp.dma_start(ent[:], self.table1[:].rearrange("(n r) w -> r n w", r=R)).then_inc(s["entries"], 16)

                    def weights(e, r):
                        sp.dma_start(wgu[:, r], ins["Wgu1"][bass.ds(e, 1)].squeeze(0)
                                     .rearrange("(c p) n -> p c n", p=P)).then_inc(s[f"w{r}"], 16)
                        sp.dma_start(wd[:, r], ins["Wd1"][bass.ds(e, 1)].squeeze(0)
                                     .rearrange("(c p) n -> p c n", p=FK)).then_inc(s[f"w{r}"], 16)
                    for r in range(WR):
                        weights(r, r)
                    with sp.Fori(0, N - 2 * WR + 1, WR) as j:
                        for r in range(WR):
                            sp.wait_ge(s["y_ready"], j + (r + 1))
                            weights(j + (r + WR), r)

            @block.gpsimd
            def _(pool):
                pool.memset(xg[:], 0.0).then_inc(s["cleared"], 1)
                pool.wait_ge(s["cleared"], 1)
                if moe == 1:
                    pool.wait_ge(s["entries"], 16)

                def gather(i, r):
                    r %= RING
                    if moe == 0:
                        pool.wait_ge(s[f"e{r}"], i * 4 + (16 - 4 * r))
                        stand_alone(pool, s["turns"])
                        src = ent[:, r:r + 1]
                    else:
                        src = ent[:, bass.ds(i, 1)]
                    pool.tensor_copy(wt[:, r:r + 1], src[:, :, 1])
                    pool.tensor_copy(sid[:, r], src.bitcast(U32)[:, :, 0]).then_inc(s["sid_ready"], 1)
                    pool.wait_ge(s["sid_ready"], i + 1)
                    stand_alone(pool, s["turns"])
                    pool.indirect_dma_start(xg[:, r], None, self.xn_dram[:],
                                            bass.IndirectOffsetOnAxis(ap=sid[:, r], axis=0),
                                            bounds_check=T - 1, oob_is_err=False).then_inc(s[f"g{r}"], 16)

                def step(i, r):
                    pool.wait_ge(s["ys_ready"], i + 1)
                    stand_alone(pool, s["turns"])
                    if not isinstance(i, int) or i > 1:
                        pool.wait_ge(s[f"scat{r % 2}"], i * 8 - 8 * (r % 2))
                        stand_alone(pool, s["turns"])
                    pool.indirect_dma_start(targets[r % 2], bass.IndirectOffsetOnAxis(ap=sid[:, r % RING], axis=0),
                                            y[:, r % 2], None, bounds_check=T - 1, oob_is_err=False,
                                            compute_op=ALU.add).then_inc(s[f"scat{r % 2}"], 16)
                    if exists(i + 3, N):
                        if not isinstance(i, int) or i > 0:
                            q = (r + 1) % 2
                            pool.wait_ge(s[f"scat{q}"], i * 8 + (8 - 8 * q))
                            stand_alone(pool, s["turns"])
                        gather(i + 3, r + 3)

                def prologue():
                    for i in range(3):
                        gather(i, i)
                pipeline(pool, N, U, prologue, step, peel_first=True)
                for q in range(2):
                    pool.wait_ge(s[f"scat{q}"], 8 * N)

            @block.tensor
            def _(pe):
                expert = {}

                def tokens(i, r):
                    r4 = r % RING
                    pe.wait_ge(s[f"g{r4}"], i * 4 + (16 - 4 * r4))
                    if not isinstance(i, int) or i > 0:
                        pe.wait_ge(s["xT_ready"], i)
                    stand_alone(pe, s["turns"])
                    for c in range(DC):
                        m = pe.transpose(ps_t[:, c * R:(c + 1) * R], xg[:, r4, c * P:(c + 1) * P], ident[0:R, 0:R])
                    m.then_inc(s["t_ready"], 1)

                def gate_up(i, r):
                    pe.wait_ge(s["xT_ready"], i + 1)
                    out = ps_g[0:R, r % 2, 0:2 * F]
                    if moe == 0:
                        stand_alone(pe, s["turns"])
                        e = pe.value_load(self.tile_expert[0:1, 0, bass.ds(i, 1)], min_val=0, max_val=E0 - 1)
                        pe.matmul(out, self.ones_bf[0:3, :], self.bias0[:, bass.ds(e, 1), 0:2 * F].squeeze(1),
                                  start=True, stop=False)
                        w = [self.wgu0[:, bass.ds(e, 1), c].squeeze(1) for c in range(DC)]
                    else:
                        pe.wait_ge(s[f"w{r % WR}"], i * 4 + (32 - 4 * (r % WR)))
                        w = [wgu[:, r % WR, c] for c in range(DC)]
                    for c in range(DC):
                        m = pe.matmul(out, xgT[:, r % 2, c], w[c], start=c == 0 and moe == 1, stop=c == DC - 1)
                    m.then_inc(s["g_ready"], 1)

                def step(i, r):
                    if exists(i + 1, N):
                        gate_up(i + 1, r + 1)
                    pe.wait_ge(s["hid_ready"], i + 1)
                    stand_alone(pe, s["turns"])
                    for c in range(2):
                        m = pe.transpose(ps_h[0:FK, c * R:(c + 1) * R], hid[:, r % 2, c * FK:(c + 1) * FK], ident[0:R, 0:R])
                    m.then_inc(s["h_ready"], 1)
                    if exists(i + 2, N):
                        tokens(i + 2, r + 2)
                    pe.wait_ge(s["hT_ready"], i + 1)
                    out = ps_y[0:R, r % 2, 0:D]
                    if moe == 0:
                        stand_alone(pe, s["turns"])
                        e = pe.value_load(self.tile_expert[0:1, 0, bass.ds(i, 1)], min_val=0, max_val=E0 - 1)
                        pe.matmul(out, self.ones_bf[0:3, :], self.bias0[:, bass.ds(e, 1), 2 * F:].squeeze(1),
                                  start=True, stop=False)
                        w = [self.wd0[:, bass.ds(e, 1), c].squeeze(1) for c in range(2)]
                    else:
                        w = [wd[:, r % WR, c] for c in range(2)]
                    for c in range(2):
                        m = pe.matmul(out, hidT[:, c], w[c], start=c == 0 and moe == 1, stop=c == 1)
                    m.then_inc(s["y_ready"], 1)

                def prologue():
                    tokens(0, 0)
                    tokens(1, 1)
                    gate_up(0, 0)
                pipeline(pe, N, U, prologue, step)

            @block.scalar
            def _(act):
                def tokens(i, r):
                    act.wait_ge(s["t_ready"], i + 1)
                    act.activation(xgT[:, r % 2], ps_t[:, 0:DC * R].rearrange("p (c r) -> p c r", c=DC), ACT.Copy)\
                        .then_inc(s["xT_ready"], 1)

                def sigmoid(i, r):
                    if moe == 0:
                        act.wait_ge(s["gate_ready"], i + 1)
                        act.activation(sig[:, r % 2], gate[:], ACT.Sigmoid, scale=1.702).then_inc(s["sig_ready"], 1)
                    else:
                        act.wait_ge(s["g_ready"], i + 1)
                        act.activation(sig[:, r % 2], ps_g[0:R, r % 2, 0:F], ACT.Sigmoid).then_inc(s["sig_ready"], 1)

                def step(i, r):
                    if exists(i + 1, N):
                        sigmoid(i + 1, r + 1)
                    act.wait_ge(s["h_ready"], i + 1)
                    act.activation(hidT[:], ps_h[0:FK, 0:2 * R].rearrange("p (c r) -> p c r", c=2), ACT.Copy)\
                        .then_inc(s["hT_ready"], 1)
                    if exists(i + 2, N):
                        tokens(i + 2, r + 2)

                def prologue():
                    tokens(0, 0)
                    tokens(1, 1)
                    sigmoid(0, 0)
                pipeline(act, N, U, prologue, step)

            @block.vector
            def _(dve):
                link = Chain(dve, s["own"])

                def activate(i, r):
                    link.begin(i * LINKS)
                    dve.wait_ge(s["g_ready"], i + 1)
                    if not isinstance(i, int) or i > 0:
                        dve.wait_ge(s["hid_ready"], i)
                    g, u = ps_g[0:R, r % 2, 0:F], ps_g[0:R, r % 2, F:2 * F]
                    if moe == 0:
                        dve.tensor_scalar(gate[:], g, 7.0, None, ALU.min).then_inc(s["gate_ready"], 1)
                        link(dve.tensor_scalar(up[:], u, 7.0, -7.0, ALU.min, ALU.max))
                        dve.wait_ge(s["sig_ready"], i + 1)
                        link(dve.tensor_tensor(glu[:], gate[:], sig[:, r % 2], ALU.mult))
                        dve.scalar_tensor_tensor(hid[:, r % 2], up[:], 1.0, glu[:], ALU.add, ALU.mult)\
                            .then_inc(s["hid_ready"], 1)
                    else:
                        dve.wait_ge(s["sig_ready"], i + 1)
                        link(dve.tensor_tensor(glu[:], g, sig[:, r % 2], ALU.mult))
                        dve.tensor_tensor(hid[:, r % 2], u, glu[:], ALU.mult).then_inc(s["hid_ready"], 1)

                def step(i, r):
                    if exists(i + 1, N):
                        activate(i + 1, r + 1)
                    dve.wait_ge(s["y_ready"], i + 1)
                    if not isinstance(i, int) or i >= 2:
                        dve.wait_ge(s[f"scat{r % 2}"], i * 8 - 8 * (r % 2))
                    dve.tensor_scalar(y[:, r % 2], ps_y[0:R, r % 2, 0:D], wt[:, r % RING:r % RING + 1], None, ALU.mult)\
                        .then_inc(s["ys_ready"], 1)
                pipeline(dve, N, U, lambda: activate(0, 0), step, peel_first=True)

    def project(self):
        nc, ins = self.nc, self.ins
        ctx, sb, ps, sem = self.scope("pj")
        W = H * DH
        with ctx:
            x = sb("x", [P, NT, D])
            wdown = sb("wdown", [P, DC, 2, P])
            wup = sb("wup", [P, 3, W])
            lnw = sb("lnw", [P, DC, 2])
            rope = sb("rope", [P, TB, 2, DH])
            stats = sb("stats", [P, 6])
            mv = sb("mv", [P, NT, 2])
            agg = sb("agg", [P, 2])
            std = sb("std", [P, NT])
            rstd = sb("rstd", [P, NT])
            mv2 = sb("mv2", [P, NT, 2])
            xn = sb("xn", [P, NT, D])
            hn = sb("hn", [P, 4, D])
            hT = sb("hT", [P, 2, DC, P])
            cT = sb("cT", [P, 2, 2, P])
            t1 = sb("t1", [P, W])
            t2 = sb("t2", [P, W])
            qkv = sb("qkv", [P, 2, 3, W])
            ps_t = ps("ps_t", [P, 512])
            ps_c = ps("ps_c", [P, 512])
            ps_u = ps("ps_u", [P, 3, W])
            names = ("turns mv_ready x0 x1 x2 x3 x_added x_out weights own std_ready std2_ready hn_ready t_ready hT_ready c_ready cT_ready "
                     "q_ready k_ready v_ready q_rot v_copied t_made q0_out q1_out xn_all").split()
            s = {n: sem(n) for n in names}
            ident = self.const("ident")
            block = ctx.enter_context(nc.Block())

            @block.sync
            def _(sp):
                for q in range(4):
                    part = slice(q * NT // 4, (q + 1) * NT // 4)
                    for dst, src in ((x, self.x_acc), (xn, self.x_odd)):
                        sp.dma_start(dst[:, part], src[:].rearrange("(n p) d -> p n d", p=P)[:, part])\
                            .then_inc(s[f"x{q}"], 16)
                for w, name in enumerate(("w_down_qT", "w_down_kvT")):
                    sp.dma_start(wdown[:, :, w], ins[name].rearrange("(c p) n -> p c n", p=P)).then_inc(s["weights"], 16)
                for w, name in enumerate(("w_up_qT", "w_up_kT", "w_up_vT")):
                    sp.dma_start(wup[:, w], ins[name]).then_inc(s["weights"], 16)
                sp.dma_start(lnw[:], ins["ln"]).then_inc(s["weights"], 16)
                sp.dma_start(rope[:], ins["rope"].rearrange("p n (w d) -> p n w d", w=2)).then_inc(s["weights"], 16)
                sp.wait_ge(s["xn_all"], 1)
                sp.dma_start(self.x_acc[:].rearrange("(n p) d -> p n d", p=P), x[:]).then_inc(s["x_out"], 16)
                for bt in range(B):
                    g0 = bt * (H // 2)
                    dst = self.qkv[g0:g0 + H // 2].rearrange("g (n p) w c -> w p n g c", p=P)
                    with sp.Fori(0, TB - 1, 2) as j:
                        for p in range(2):
                            sp.wait_ge(s["q_rot"], j * 2 + (2 * bt * TB + 2 * p + 2))
                            stand_alone(sp, s["turns"])
                            sp.wait_ge(s["v_copied"], j + (bt * TB + p + 2))
                            stand_alone(sp, s["turns"])
                            for w in range(3):
                                sp.dma_start(dst[w][:, bass.ds(j + p, 1)].squeeze(1),
                                             qkv[:, p, w].rearrange("p (g c) -> p g c", c=P))\
                                    .then_inc(s[f"q{p}_out"], 16)
                sp.wait_ge(s["x_out"], 16)
                sp.wait_ge(s["q0_out"], 24 * NT + 48)
                sp.wait_ge(s["q1_out"], 24 * NT + 48)

            @block.vector
            def _(dve):
                link = Chain(dve, s["own"])
                for q in range(4):
                    part = slice(q * NT // 4, (q + 1) * NT // 4)
                    dve.wait_ge(s[f"x{q}"], 32)
                    dve.tensor_tensor(x[:, part], x[:, part], xn[:, part], ALU.add).then_inc(s["x_added"], 1)
                    dve.wait_ge(s["x_added"], q + 1)
                    self.statistics(dve, link, s, x, stats, agg, mv, q * NT // 4, (q + 1) * NT // 4)
                dve.wait_ge(s["std_ready"], 1)
                link.begin(2 * NT)
                link(dve.reciprocal(rstd[:], std[:]))
                with dve.Fori(0, NT) as i:
                    link.begin(i * 3 + (2 * NT + 1))
                    link(dve.tensor_scalar(xn[:, bass.ds(i, 1), :].squeeze(1), x[:, bass.ds(i, 1), :].squeeze(1),
                                           mv[:, bass.ds(i, 1), 0], rstd[:, bass.ds(i, 1)],
                                           ALU.subtract, ALU.mult))
                    stand_alone(dve, s["turns"])
                    link(dve.bn_stats(stats[:], xn[:, bass.ds(i, 1), :].squeeze(1)))
                    stand_alone(dve, s["turns"])
                    link(dve.bn_aggr(agg[:], stats[:]))
                    dve.tensor_copy(mv2[:, bass.ds(i, 1), :].squeeze(1), agg[:]).then_inc(s["mv_ready"], 1)
                dve.wait_ge(s["std2_ready"], 1)
                link.begin(5 * NT + 1)
                link(dve.reciprocal(rstd[:], std[:]))
                dve.tensor_tensor(x[:], x[:], xn[:], ALU.add).then_inc(s["xn_all"], 1)
                dve.wait_ge(s["weights"], 16 * 7)

                def tokens(i, r):
                    dve.tensor_scalar(hn[:, r % 4], xn[:, bass.ds(i, 1), :].squeeze(1), mv2[:, bass.ds(i, 1), 0],
                                      rstd[:, bass.ds(i, 1)], ALU.subtract, ALU.mult).then_inc(s["hn_ready"], 1)

                def back(i, b, p):
                    dve.wait_ge(s[f"q{p}_out"], i * 24 + (48 if p == 0 else 24))
                    for w, ready in enumerate(("q_ready", "k_ready")):
                        dve.wait_ge(s[ready], i + 1)
                        src = ps_u[:, w].rearrange("p (h e r) -> p h e r", h=H, e=2)
                        cs = rope[:, bass.ds(b, 1), 0, :].broadcast_to([P, H, DH]).rearrange("p h (e r) -> p h e r", e=2)
                        sn = rope[:, bass.ds(b, 1), 1, :].broadcast_to([P, H, DH]).rearrange("p h (e r) -> p h e r", e=2)
                        a = t1[:].rearrange("p (h e r) -> p h e r", h=H, e=2)
                        c = t2[:].rearrange("p (h e r) -> p h e r", h=H, e=2)
                        dve.tensor_tensor(a, src, cs, ALU.mult)
                        dve.tensor_tensor(c[:, :, 0], src[:, :, 1], sn[:, :, 0], ALU.mult)
                        dve.tensor_tensor(c[:, :, 1], src[:, :, 0], sn[:, :, 1], ALU.mult).then_inc(s["t_made"], 1)
                        dve.wait_ge(s["t_made"], i * 2 + (w + 3))
                        dve.tensor_tensor(qkv[:, p, w], t1[:], t2[:], ALU.add).then_inc(s["q_rot"], 1)
                        dve.wait_ge(s["q_rot"], i * 2 + (w + 1))

                for i in range(3):
                    tokens(i, i)
                for bt in range(B):
                    base = bt * TB
                    last = TB - (4 if bt == B - 1 else 0)
                    with dve.Fori(0, last - 3, 4) as j:
                        for r in range(4):
                            tokens(j + (base + r + 3), r + 3)
                            back(j + (base + r), j + r, r % 2)
                    for r in range(last, TB):
                        if base + r + 3 < NT:
                            tokens(base + r + 3, r + 3)
                        back(base + r, r, r % 2)

            @block.scalar
            def _(act):
                act.sem_inc(s["q0_out"], 48)
                act.sem_inc(s["q1_out"], 48)
                act.wait_ge(s["mv_ready"], NT)
                act.activation(std[:], mv[:, :, 1], ACT.Sqrt, bias=self.eps[:, 0:1]).then_inc(s["std_ready"], 1)
                act.wait_ge(s["mv_ready"], 2 * NT)
                act.activation(std[:], mv2[:, :, 1], ACT.Sqrt, bias=self.eps[:, 0:1]).then_inc(s["std2_ready"], 1)
                act.wait_ge(s["weights"], 16 * 7)

                def tokens(i, r):
                    act.wait_ge(s["t_ready"], i + 1)
                    for c in range(DC):
                        m = act.activation(hT[:, r % 2, c], ps_t[:, c * P:(c + 1) * P], ACT.Identity,
                                           bias=lnw[:, c, 1:2], scale=lnw[:, c, 0:1])
                    m.then_inc(s["hT_ready"], 1)

                def down(i, r):
                    act.wait_ge(s["c_ready"], i + 1)
                    act.activation(cT[:, r % 2], ps_c[:, 0:2 * P].rearrange("p (w l) -> p w l", w=2), ACT.Copy)\
                        .then_inc(s["cT_ready"], 1)

                def step(i, r):
                    if exists(i + 2, NT):
                        tokens(i + 2, r + 2)
                    if exists(i + 1, NT):
                        down(i + 1, r + 1)
                    p = r % 2
                    act.wait_ge(s["v_ready"], i + 1)
                    act.wait_ge(s[f"q{p}_out"], i * 24 + (48 if p == 0 else 24))
                    act.activation(qkv[:, p, 2], ps_u[:, 2], ACT.Copy).then_inc(s["v_copied"], 1)

                def prologue():
                    tokens(0, 0)
                    tokens(1, 1)
                    down(0, 0)
                pipeline(act, NT, 2, prologue, step)

            @block.tensor
            def _(pe):
                pe.sem_inc(s["t_made"], 2)
                pe.sem_inc(s["v_copied"], 1)
                pe.wait_ge(s["weights"], 16 * 7)

                def tokens(i, r):
                    pe.wait_ge(s["hn_ready"], i + 1)
                    if not isinstance(i, int) or i > 0:
                        pe.wait_ge(s["hT_ready"], i)
                    for c in range(DC):
                        m = pe.transpose(ps_t[:, c * P:(c + 1) * P], hn[:, r % 4, c * P:(c + 1) * P], ident)
                    m.then_inc(s["t_ready"], 1)

                def down(i, r):
                    pe.wait_ge(s["hT_ready"], i + 1)
                    for w in range(2):
                        for c in range(DC):
                            m = pe.matmul(ps_c[:, w * P:(w + 1) * P], wdown[:, c, w], hT[:, r % 2, c],
                                          start=c == 0, stop=c == DC - 1)
                    m.then_inc(s["c_ready"], 1)

                def step(i, r):
                    pe.wait_ge(s["cT_ready"], i + 1)
                    if exists(i + 2, NT):
                        tokens(i + 2, r + 2)
                    if exists(i + 1, NT):
                        down(i + 1, r + 1)
                    for w, (ready, src, free, value) in enumerate((
                            ("q_ready", 0, "t_made", i * 2 + 1), ("k_ready", 1, "t_made", i * 2 + 2),
                            ("v_ready", 1, "v_copied", i + 1))):
                        pe.wait_ge(s[free], value)
                        for h in range(W // 512):
                            m = pe.matmul(ps_u[:, w, h * 512:(h + 1) * 512], cT[:, r % 2, src],
                                          wup[:, w, h * 512:(h + 1) * 512], start=True, stop=True)
                        m.then_inc(s[ready], 1)

                def prologue():
                    tokens(0, 0)
                    tokens(1, 1)
                    down(0, 0)
                pipeline(pe, NT, 4, prologue, step)

    def softmax_attention(self):
        nc = self.nc
        NG = NQB
        NU = (L // P) * (L // QB)
        items = [("K", g) for g in range(NG)] + [("Q", g) for g in range(NG)]
        for u in range(NU):
            items.append(("U", u))
            if u % 16 == 4 and u > 16:
                items.append(("M", u // 16 - 1))
        items.append(("M", NG - 1))
        NI = len(items)
        SLOTS = NQB * KC // 2
        plan = [items[2 * n:2 * n + 2] for n in range(4)] + [items[8 + 3 * n:min(11 + 3 * n, NI - 1)] for n in range(23)]
        plan += [[], [], items[NI - 1:], [], []]
        assert len(plan) == SLOTS and sum(plan, []) == items and NI % 2 == 0
        HEADS = B * H
        MROW, MROW2 = DH, DH + 32
        ctx, sb, ps, sem = self.scope("at")
        with ctx:
            kd = sb("kd", [P, 2, KC, 2, DH])
            qd = sb("qd", [P, 2, KC, 2, DH])
            v1 = sb("v1", [P, 2, KC, 2 * DH])
            k1 = [sb(f"k1_{i}", [P, L], F32R) for i in range(2)]
            k2 = [sb(f"k2_{i}", [P, L], F32R) for i in range(2)]
            q1 = [sb(f"q1_{i}", [P, L], F32R) for i in range(2)]
            q2 = [sb(f"q2_{i}", [P, L], F32R) for i in range(2)]
            mx = sb("mx", [P, NU])
            mg = sb("mg", [P, KC])
            nm = sb("nm", [P, KC])
            NP = 4
            pr_ = sb("prob", [P, NP, 2 * QB])
            rc = sb("rc", [DH, QB])
            PIECES = 4
            o_st = sb("o_st", [DH, 2, QB])
            ps_s = ps("ps_s", [P, 2, 2 * QB])
            ps_v = ps("ps_v", [P, 2, QB])
            ps_r = ps("ps_r", [P, 2, QB])
            names = ("turns kd0 kd1 qd0 qd1 v0 v1 fixed ring_full ring_free own k1_ready k_copied q1_ready nm_ready "
                     "q2_ready s_full p_ready pv_done rc_ready o_ready o0_out o1_out").split()
            s = {n: sem(n) for n in names}
            ident = self.const("ident")
            block = ctx.enter_context(nc.Block())

            def all_heads(step, first):
                first()
                return step

            @block.sync
            def _(sp):
                def load_qk(pr, hh):
                    for d, name, w in ((kd, "kd", 1), (qd, "qd", 0)):
                        src = self.qkv[bass.ds(pr, 1), :, w, hh * DH:(hh + 1) * DH].squeeze(0)\
                            .rearrange("(n p) c -> p n c", p=P)
                        for twice in range(2):
                            sp.dma_start(d[:, hh, :, twice, :], src).then_inc(s[f"{name}{hh}"], 16)

                def load_v(pr, hh):
                    src = self.qkv[bass.ds(pr, 1), :, 2, hh * DH:(hh + 1) * DH].squeeze(0)\
                        .rearrange("(n p) c -> p n c", p=P)
                    sp.dma_start(v1[:, hh, :, 0:DH], src).then_inc(s[f"v{hh}"], 16)

                def store_o(pr, hh):
                    for qb in range(NQB):
                        sp.wait_ge(s["o_ready"], pr * (2 * NQB) + (hh * NQB + qb + 3))
                        sp.dma_start(self.o_dram[bass.ds(pr, 1), hh * DH:(hh + 1) * DH, qb * QB:(qb + 1) * QB].squeeze(0),
                                     o_st[:, qb % 2]).then_inc(s[f"o{qb % 2}_out"], 16)

                load_qk(0, 0)
                load_qk(0, 1)
                load_v(0, 0)
                load_v(0, 1)
                with sp.Fori(0, PAIRS - 1) as pr:
                    for hh in range(2):
                        sp.wait_ge(s["ring_full"], pr * (2 * NI) + (hh * NI + 8))
                        load_qk(pr + 1, hh)
                        store_o(pr, hh)
                        sp.wait_ge(s["pv_done"], pr * (2 * SLOTS) + (hh * SLOTS + SLOTS + NP))
                        load_v(pr + 1, hh)
                for hh in range(2):
                    store_o(PAIRS - 1, hh)
                for ob in range(2):
                    sp.wait_ge(s[f"o{ob}_out"], 16 + 16 * HEADS * NQB // 2)

            @block.gpsimd
            def _(pool):
                link = Chain(pool, s["fixed"])
                link(pool.memset(v1[:, :, :, DH:], 1.0))
                for i in range(2):
                    link(pool.memset(k2[i][DH:P, :].bitcast(F32), 0.0))
                    link(pool.memset(q2[i][DH:P, :].bitcast(F32), 0.0))
                    for r in (MROW, MROW2):
                        link(pool.memset(k2[i][r:r + 1, :].bitcast(F32), 1.0))

                def keys(pr, hh):
                    for g in range(NG):
                        at = slice(g * QB, (g + 1) * QB)
                        pool.wait_ge(s["k1_ready"], pr * (2 * NG) + (hh * NG + g + 1))
                        stand_alone(pool, s["turns"])
                        pool.tensor_copy(k2[hh][0:DH, at], k1[hh][0:DH, at]).then_inc(s["k_copied"], 1)
                with pool.Fori(0, PAIRS) as pr:
                    for hh in range(2):
                        keys(pr, hh)

            @block.vector
            def _(dve):
                link = Chain(dve, s["own"])
                LH = 2 * NG + 2 * NG + NG + NG
                dve.sem_inc(s["ring_free"], 2)
                dve.sem_inc(s["o_ready"], 2)
                dve.sem_inc(s["o0_out"], 16)
                dve.sem_inc(s["o1_out"], 16)
                dve.wait_ge(s["fixed"], 9)
                count = {"c": 0}

                def item(pr, hh, kind, n, index, base):
                    dve.wait_ge(s["ring_full"], base * NI + (index + 1))
                    bank = ps_r[:, index % 2]
                    at = slice(n * QB, (n + 1) * QB)
                    if kind == "K":
                        dve.tensor_copy(k1[hh][:, at], bank).then_inc(s["k1_ready"], 1)
                        dve.wait_ge(s["k1_ready"], base * NG + (n + 1))
                        low = k1[hh][DH:P, at]
                        dve.tensor_tensor(low, bank[DH:P], low.bitcast(F32), ALU.subtract).then_inc(s["ring_free"], 1)
                    elif kind == "Q":
                        dve.tensor_copy(q1[hh][:, at], bank).then_inc(s["q1_ready"], 1)
                        dve.wait_ge(s["q1_ready"], base * NG + (n + 1))
                        dve.tensor_tensor(q2[hh][0:DH, at], bank[0:DH], q1[hh][0:DH, at].bitcast(F32), ALU.subtract)\
                            .then_inc(s["ring_free"], 1)
                    elif kind == "U":
                        dve.tensor_reduce(mx[:, n:n + 1], bank, X, ALU.max).then_inc(s["ring_free"], 1)
                        if n % 16 == 15:
                            g = n // 16
                            dve.wait_ge(s["ring_free"], base * NI + (index + 3))
                            mxv = mx[:, n - 15:n + 1].rearrange("p (t k) -> p t k", k=4)
                            own(base, dve.tensor_reduce(mg[:, 4 * g:4 * g + 4], mxv, X, ALU.max))
                            dve.tensor_scalar(nm[:, 4 * g:4 * g + 4], mg[:, 4 * g:4 * g + 4], -1.0, None, ALU.mult)\
                                .then_inc(s["nm_ready"], 1)
                    else:
                        own(base, dve.tensor_copy(q2[hh][MROW:MROW + 1, at], bank[0:1]))
                        dve.tensor_tensor(q2[hh][MROW2:MROW2 + 1, at], bank[0:1],
                                          q2[hh][MROW:MROW + 1, at].bitcast(F32), ALU.subtract)\
                            .then_inc(s["ring_free"], 1)
                        dve.wait_ge(s["ring_free"], base * NI + (index + 3))
                        dve.sem_inc(s["q2_ready"], 1)

                def own(base, ins_):
                    count["c"] += 1
                    ins_.then_inc(s["own"], 1)
                    dve.wait_ge(s["own"], base * (2 * NG) + count["c"])

                def output(g, qb, piece):
                    if piece == 0:
                        dve.wait_ge(s["pv_done"], g * SLOTS + ((qb + 1) * 8 + NP))
                    if piece < PIECES:
                        at = slice(piece * QB // PIECES, (piece + 1) * QB // PIECES)
                        dve.reciprocal(rc[:, at], ps_v[DH:P, qb % 2, at]).then_inc(s["rc_ready"], 1)
                        return
                    dve.wait_ge(s["rc_ready"], g * (PIECES * NQB) + (PIECES * (qb + 1)))
                    dve.wait_ge(s[f"o{qb % 2}_out"], g * 32 + (16 * (qb // 2) + 16))
                    dve.tensor_tensor(o_st[:, qb % 2], ps_v[0:DH, qb % 2], rc[:], ALU.mult).then_inc(s["o_ready"], 1)
                    dve.wait_ge(s["o_ready"], g * NQB + (qb + 3))

                def head(pr, hh, prepare):
                    g = pr * 2 + hh
                    nxt = pr * 2 + (hh + 1)
                    count["c"] = 0
                    index = 0
                    for n in range(SLOTS):
                        if n >= 8 and 1 <= n % 8 <= PIECES + 1:
                            output(g, n // 8 - 1, n % 8 - 1)
                        if prepare:
                            for kind, m in plan[n]:
                                item(pr, 1 - hh, kind, m, index, nxt)
                                index += 1
                    for piece in range(PIECES + 1):
                        output(g, NQB - 1, piece)

                for index, (kind, m) in enumerate(items):
                    item(0, 0, kind, m, index, 0)
                with dve.Fori(0, PAIRS - 1) as pr:
                    head(pr, 0, True)
                    head(pr, 1, True)
                head(PAIRS - 1, 0, True)
                head(PAIRS - 1, 1, False)

            @block.scalar
            def _(act):
                act.sem_inc(s["pv_done"], NP)
                with act.Fori(0, PAIRS) as pr:
                    for n in range(2 * SLOTS):
                        act.wait_ge(s["s_full"], pr * (2 * SLOTS) + (n + 1))
                        act.wait_ge(s["pv_done"], pr * (2 * SLOTS) + (n + 1))
                        act.activation(pr_[:, n % NP], ps_s[:, n % 2], ACT.Exp, scale=DH ** -0.5)\
                            .then_inc(s["p_ready"], 1)

            @block.tensor
            def _(pe):
                pe.wait_ge(s["fixed"], 9)

                def item(hh, kind, n, index, base, half):
                    pe.wait_ge(s["ring_free"], base * NI + (index + 1))
                    bank = ps_r[:, index % 2]
                    if kind in "KQ":
                        src, name = (kd, "kd") if kind == "K" else (qd, "qd")
                        if n == 0:
                            pe.wait_ge(s[f"{name}{hh}"], half * 32 + 32)
                        for t in range(4):
                            m = pe.transpose(bank[:, t * P:(t + 1) * P],
                                             src[:, hh, 4 * n + t].rearrange("p w c -> p (w c)"), ident)
                    elif kind == "U":
                        if n == 0:
                            pe.wait_ge(s["ring_free"], base * NI + 10)
                        t, kb = n // 4, n % 4
                        m = pe.matmul(bank, q1[hh][:, t * P:(t + 1) * P], k1[hh][:, kb * QB:(kb + 1) * QB],
                                      start=True, stop=True)
                    else:
                        pe.wait_ge(s["nm_ready"], base * NG + (n + 1))
                        for t in range(4):
                            m = pe.transpose(bank[0:1, t * P:(t + 1) * P], nm[:, 4 * n + t:4 * n + t + 1], ident)
                    m.then_inc(s["ring_full"], 1)

                def scores(g, hh, n, j):
                    qb, c2 = n // 8, n % 8
                    if c2 == 0 and j == 0:
                        pe.wait_ge(s["q2_ready"], g * NG + (qb + 1))
                        if qb == 0:
                            pe.wait_ge(s["k_copied"], g * NG + NG)
                    c = 2 * c2 + j
                    ks, qs = slice(c * P, (c + 1) * P), slice(qb * QB, (qb + 1) * QB)
                    out = ps_s[:, n % 2, j * QB:(j + 1) * QB]
                    pe.matmul(out, k1[hh][:, ks], q1[hh][:, qs], start=True, stop=False)
                    m = pe.matmul(out, k2[hh][:, ks], q2[hh][:, qs], start=False, stop=True)
                    if j == 1:
                        m.then_inc(s["s_full"], 1)

                def values(g, hh, n, half, j):
                    qb, c2 = n // 8, n % 8
                    if j == 0:
                        if n == 0:
                            pe.wait_ge(s[f"v{hh}"], half * 16 + 16)
                        if c2 == 0:
                            pe.wait_ge(s["o_ready"], g * NQB + (qb + 1))
                        pe.wait_ge(s["p_ready"], g * SLOTS + (n + 1))
                    c = 2 * c2 + j
                    m = pe.matmul(ps_v[:, qb % 2], v1[:, hh, c], pr_[:, n % NP, j * QB:(j + 1) * QB],
                                  start=c == 0, stop=c == KC - 1)
                    if j == 1:
                        m.then_inc(s["pv_done"], 1)

                def head(pr, hh, prepare):
                    g, nxt = pr * 2 + hh, pr * 2 + (hh + 1)
                    index = 0
                    for n in range(SLOTS):
                        work = list(plan[n]) if prepare else []
                        scores(g, hh, n, 0)
                        if work:
                            item(1 - hh, *work.pop(0), index, nxt, pr + hh)
                            index += 1
                        scores(g, hh, n, 1)
                        for j in range(2):
                            if n > 0:
                                values(g, hh, n - 1, pr, j)
                            if work:
                                item(1 - hh, *work.pop(0), index, nxt, pr + hh)
                                index += 1
                    for j in range(2):
                        values(g, hh, SLOTS - 1, pr, j)

                for index, (kind, m) in enumerate(items):
                    item(0, kind, m, index, 0, 0)
                with pe.Fori(0, PAIRS - 1) as pr:
                    head(pr, 0, True)
                    head(pr, 1, True)
                head(PAIRS - 1, 0, True)
                head(PAIRS - 1, 1, False)

    def output_projection(self):
        nc, ins, x = self.nc, self.ins, self.x
        ctx, sb, ps, sem = self.scope("op")
        G = H // 2
        with ctx:
            wo = sb("wo", [P, G, D])
            oT = sb("oT", [P, 4, G, P])
            ps_o = ps("ps_o", [P, 2, 512])
            s = {n: sem(n) for n in "x weights o0 o1 o2 o3 out_ready added".split()}
            block = ctx.enter_context(nc.Block())

            @block.sync
            def _(sp):
                sp.dma_start(wo[:], ins["w_outT"].rearrange("(g p) n -> p g n", p=P)).then_inc(s["weights"], 16)
                sp.dma_start(x[:], self.x_acc[:].rearrange("(n p) d -> p n d", p=P)).then_inc(s["x"], 16)
                for b in range(B):
                    src = self.o_dram[b * G:(b + 1) * G].rearrange("g p (n l) -> p n g l", l=P)

                    def load(j, r):
                        sp.dma_start(oT[:, r], src[:, bass.ds(j + r, 1)].squeeze(1)).then_inc(s[f"o{r}"], 16)
                    if b == 0:
                        for r in range(4):
                            load(0, r)
                    with sp.Fori(4 if b == 0 else 0, TB - 3, 4) as j:
                        for r in range(4):
                            sp.wait_ge(s["out_ready"], j + (b * TB - 4 + r + 1))
                            load(j, r)

            @block.tensor
            def _(pe):
                pe.wait_ge(s["weights"], 16)
                pe.sem_inc(s["added"], 2)
                with pe.Fori(0, NT - 3, 4) as j:
                    for r in range(4):
                        pe.wait_ge(s[f"o{r}"], j * 4 + 16)
                        pe.wait_ge(s["added"], j + (r + 1))
                        for g in range(G):
                            m = pe.matmul(ps_o[:, r % 2, 0:D], oT[:, r, g], wo[:, g], start=g == 0, stop=g == G - 1)
                        m.then_inc(s["out_ready"], 1)

            @block.vector
            def _(dve):
                dve.wait_ge(s["x"], 16)
                with dve.Fori(0, NT - 1, 2) as j:
                    for r in range(2):
                        dve.wait_ge(s["out_ready"], j + (r + 1))
                        dve.tensor_tensor(x[:, bass.ds(j + r, 1)].squeeze(1), ps_o[:, r, 0:D],
                                          x[:, bass.ds(j + r, 1)].squeeze(1), ALU.add).then_inc(s["added"], 1)

    def add_odd(self):
        nc = self.nc
        ctx, sb, ps, sem = self.scope("ao")
        QUARTERS = 4
        with ctx:
            even = sb("even", [P, NT, D])
            odd = sb("odd", [P, NT, D])
            s = {n: sem(n) for n in "in0 in1 in2 in3 added stored".split()}
            block = ctx.enter_context(nc.Block())

            def part(q, of=None):
                tiles = slice(q * NT // QUARTERS, (q + 1) * NT // QUARTERS)
                return tiles if of is None else of.rearrange("(n p) d -> p n d", p=P)[:, tiles]

            @block.sync
            def _(sp):
                for q in range(QUARTERS):
                    sp.dma_start(even[:, part(q)], part(q, self.out)).then_inc(s[f"in{q}"], 16)
                    sp.dma_start(odd[:, part(q)], part(q, self.out_odd[:])).then_inc(s[f"in{q}"], 16)
                for q in range(QUARTERS):
                    sp.wait_ge(s["added"], q + 1)
                    sp.dma_start(part(q, self.out), even[:, part(q)]).then_inc(s["stored"], 16)
                sp.wait_ge(s["stored"], 16 * QUARTERS)

            @block.vector
            def _(dve):
                for q in range(QUARTERS):
                    dve.wait_ge(s[f"in{q}"], 32)
                    dve.tensor_tensor(even[:, part(q)], even[:, part(q)], odd[:, part(q)], ALU.add)\
                        .then_inc(s["added"], 1)


def kernel(L0_attn_X, L0_attn_Wq, L0_attn_Wv, L0_attn_q_norm_w, L0_attn_v_norm_w, L0_ffn_Wg, L0_ffn_bg,
           L0_ffn_Wgu, L0_ffn_bgu, L0_ffn_Wd, L0_ffn_bd, L1_attn_w_down_q, L1_attn_w_down_kv, L1_attn_w_up_q,
           L1_attn_w_up_k, L1_attn_w_up_v, L1_attn_w_out, L1_attn_ln_scale, L1_attn_ln_bias, L1_ffn_gate_w,
           L1_ffn_w_gate, L1_ffn_w_up, L1_ffn_w_down):
    import concourse.bacc as bacc
    from concourse.bass_utils import run_bass_kernel_spmd

    def halves(w):
        w = np.asarray(w).reshape(H, HALF, 2, P).transpose(0, 2, 1, 3).reshape(H * DH, P)
        return w.T

    def deinterleave(w):
        w = np.asarray(w)
        return np.concatenate([w[..., ::2], w[..., 1::2]], -1)

    def ln_columns(v):
        return np.asarray(v).reshape(DC, P).T
    arrays = {
        "X": np.asarray(L0_attn_X).reshape(T, D),
        "consts": shape_constants(), "rope": rope_constants(),
        "WqT": np.asarray(L0_attn_Wq).T, "WvT": np.asarray(L0_attn_Wv).T,
        "qw": np.asarray(L0_attn_q_norm_w).reshape(-1), "vw": np.asarray(L0_attn_v_norm_w).reshape(-1),
        "router0": np.asarray(L0_ffn_Wg).T, "bg": np.asarray(L0_ffn_bg),
        "Wgu": deinterleave(L0_ffn_Wgu), "bgu": deinterleave(L0_ffn_bgu),
        "Wd": np.asarray(L0_ffn_Wd), "bd": np.asarray(L0_ffn_bd),
        "w_down_qT": np.asarray(L1_attn_w_down_q).T, "w_down_kvT": np.asarray(L1_attn_w_down_kv).T,
        "w_up_qT": halves(L1_attn_w_up_q), "w_up_kT": halves(L1_attn_w_up_k),
        "w_up_vT": np.asarray(L1_attn_w_up_v).T, "w_outT": np.asarray(L1_attn_w_out).T,
        "ln": np.stack([ln_columns(L1_attn_ln_scale), ln_columns(L1_attn_ln_bias)], -1),
        "router1": np.asarray(L1_ffn_gate_w).T,
        "Wgu1": np.concatenate([np.asarray(L1_ffn_w_gate), np.asarray(L1_ffn_w_up)], 1).transpose(0, 2, 1),
        "Wd1": np.asarray(L1_ffn_w_down).transpose(0, 2, 1),
    }
    arrays = {k: np.ascontiguousarray(v) for k, v in arrays.items()}
    nc = bacc.Bacc("TRN2", target_bir_lowering=False, num_devices=1)
    ins = {k: nc.dram_tensor(k + "_in", v.shape, mybir.dt.from_np(v.dtype), kind="ExternalInput").ap()
           for k, v in arrays.items()}
    out = nc.dram_tensor("out", (T, D), F32, kind="ExternalOutput").ap()
    Kernel(nc, ins, out).build()
    r = run_bass_kernel_spmd(nc, [{k + "_in": v for k, v in arrays.items()}], core_ids=[0])
    return r.results[0]["out"].reshape(B, L, D)
```

```python
import numpy as np
import concourse.bass as bass
from concourse import mybir
from contextlib import ExitStack

F32 = mybir.dt.float32
F32R = mybir.dt.float32r
BF16 = mybir.dt.bfloat16
U32 = mybir.dt.uint32
ACT = mybir.ActivationFunctionType
ALU = mybir.AluOpType
X = mybir.AxisListType.X

B, L, D = 2, 2048, 256
T = B * L
P = 128
NT = T // P
TB = L // P
DC = D // P
H0, D0 = 16, 16
H, DH = 16, 64
PAIRS = B * H // 2
QB = 512
NQB = L // QB
KC = L // P
E0, K0, F0 = 16, 2, 256
E1, K1_, F1 = 64, 8, 192
CAP = 64
ST0 = T * K0 // P + E0 - 1
BLOCKS0 = E0 * NT + 1
LN_EPS = 1e-5
RMS_EPS = 1e-8
DROP = 1 << 20
HALF = DH // 2

CONST = [("ident", P), ("causal", P), ("before", P), ("blocks", P), ("parity", 2), ("keep", NT),
         ("iota", E1), ("token", NT), ("tiles", ST0 + 1)]


def const_at(name):
    at = 0
    for n, w in CONST:
        if n == name:
            return at, at + w
        at += w
    raise KeyError(name)


def shape_constants():
    c = np.zeros((P, sum(w for _, w in CONST)), np.float32)
    r = np.arange(P)

    def put(name, value):
        a, b = const_at(name)
        c[:, a:b] = value
    put("ident", np.eye(P))
    put("causal", r[:, None] <= r[None, :])
    put("before", r[:, None] < r[None, :])
    put("blocks", r[:, None] // D0 == r[None, :] // D0)
    put("parity", np.stack([(r // D0) % 2 == 0, (r // D0) % 2 == 1], 1))
    put("keep", (np.arange(NT) % TB != TB - 1)[None, :])
    put("iota", np.arange(E1)[None, :])
    put("token", (np.arange(NT)[None, :] * P + r[:, None]))
    put("tiles", np.arange(ST0 + 1)[None, :])
    return c


def rope_constants():
    inv = 1.0 / 10000.0 ** (np.arange(0, DH, 2, dtype=np.float32) / DH)
    f = np.outer(np.arange(L, dtype=np.float32), inv)
    cos = np.concatenate([np.cos(f), np.cos(f)], -1)[:, ::2]
    sin = np.concatenate([np.sin(f), np.sin(f)], -1)[:, ::2]
    t = np.stack([np.concatenate([cos, cos], 1), np.concatenate([-sin, sin], 1)], 1)
    return np.ascontiguousarray(t.reshape(TB, P, 2 * DH).transpose(1, 0, 2)).astype(np.float32)


class Chain:

    def __init__(self, eng, sem):
        self.eng, self.sem, self.base, self.n = eng, sem, 0, 0

    def __call__(self, ins):
        self.n += 1
        ins.then_inc(self.sem, 1)
        self.eng.wait_ge(self.sem, self.base + self.n)

    def begin(self, base):
        self.base, self.n = base, 0


def pipeline(eng, n, unroll, prologue, step, peel_first=False):
    prologue()
    if peel_first:
        for r in range(unroll):
            step(r, r)
    with eng.Fori(unroll if peel_first else 0, n - 2 * unroll + 1, unroll) as j:
        for r in range(unroll):
            step(j + r, r)
    for r in range(unroll):
        step(n - unroll + r, r)


def exists(i, n):
    return not isinstance(i, int) or i < n


def stand_alone(eng, turns):
    eng.sem_inc(turns, 1)


class Kernel:
    def __init__(self, nc, ins, out):
        self.nc, self.ins, self.out = nc, ins, out
        self.sems = 0

    def build(self):
        nc = self.nc
        self.x_acc = nc.dram_tensor("x_acc", (T, D), F32)
        self.x_odd = nc.dram_tensor("x_odd", (T, D), F32)
        self.out_odd = nc.dram_tensor("out_odd", (T, D), F32)
        self.xn_dram = nc.dram_tensor("xn_dram", (T, D), F32)
        self.table0 = nc.dram_tensor("table0", (BLOCKS0 * P, 2), F32)
        self.table1 = nc.dram_tensor("table1", (E1 * CAP, 2), F32)
        self.qkv = nc.dram_tensor("qkv", (PAIRS, L, 3, P), F32)
        self.o_dram = nc.dram_tensor("o_dram", (PAIRS, P, L), F32)
        self.den = nc.dram_tensor("den", (PAIRS, 2, L), F32)
        self.rden = nc.dram_tensor("rden", (PAIRS, 2, L), F32)
        with ExitStack() as keep:
            self.C = keep.enter_context(nc.sbuf_tensor("C", [P, sum(w for _, w in CONST)], F32))
            self.tri = keep.enter_context(nc.sbuf_tensor("tri", [P, P], BF16))
            self.ones_bf = keep.enter_context(nc.sbuf_tensor("ones_bf", [P, P], BF16))
            self.eps = keep.enter_context(nc.sbuf_tensor("eps", [P, 2], F32))
            with ExitStack() as xs:
                self.x = xs.enter_context(nc.sbuf_tensor("x_sb", [P, NT, D], F32))
                self.mv = xs.enter_context(nc.sbuf_tensor("mv_sb", [P, NT, 2], F32))
                self.linear_attention()
                with ExitStack() as moe0:
                    self.tile_expert = moe0.enter_context(nc.sbuf_tensor("tile_expert", [1, 2, ST0 + 1], U32))
                    self.wgu0 = moe0.enter_context(nc.sbuf_tensor("wgu0", [P, E0, DC, 2 * F0], F32))
                    self.wd0 = moe0.enter_context(nc.sbuf_tensor("wd0", [P, E0, DC, D], F32))
                    self.bias0 = moe0.enter_context(nc.sbuf_tensor("bias0", [3, E0, 2 * F0 + D], BF16))
                    self.route(0, E0, K0, self.table0, self.x_acc[:])
                    self.experts(0)
            self.project()
            self.softmax_attention()
            with ExitStack() as xs:
                self.x = xs.enter_context(nc.sbuf_tensor("x_sb2", [P, NT, D], F32))
                self.mv = xs.enter_context(nc.sbuf_tensor("mv_sb2", [P, NT, 2], F32))
                self.output_projection()
                self.route(1, E1, K1_, self.table1, self.out)
            self.experts(1)
            self.add_odd()

    def const(self, name):
        a, b = const_at(name)
        return self.C[:, a:b]

    def scope(self, stage):
        ctx, nc = ExitStack(), self.nc
        sb = lambda name, shape, dt=F32: ctx.enter_context(nc.sbuf_tensor(f"{stage}_{name}", shape, dt))
        ps = lambda name, shape, dt=F32: ctx.enter_context(nc.psum_tensor(f"{stage}_{name}", shape, dt))
        held = []

        def sem(name):
            held.append(nc.alloc_semaphore(f"{stage}_{name}"))
            return held[-1]

        def release():
            nc.clear_and_free_semaphores(held)
            nc.all_engine_barrier()
        ctx.callback(release)
        return ctx, sb, ps, sem

    def linear_attention(self):
        nc, ins, x = self.nc, self.ins, self.x
        ctx, sb, ps, sem = self.scope("la")
        with ctx:
            wqv = sb("wqv", [P, DC, 2 * D])
            normw = sb("normw", [P, 2 * D])
            stats = sb("stats", [P, 6])
            mv = sb("mv", [P, 4, 2])
            std = sb("std", [P, 4])
            rstd = sb("rstd", [P, 4])
            agg = sb("agg", [P, 2])
            xn = sb("xn", [P, 4, D])
            xnT = sb("xnT", [P, 4, D])
            sq = sb("sq", [P, 2 * D])
            ss = sb("ss", [P, 2 * H0])
            rt = sb("rt", [P, 2 * H0])
            rr = sb("rr", [P, 2 * H0])
            qv1 = sb("qv1", [P, 2 * D])
            qv = sb("qv", [P, 4, 2 * D])
            qz = sb("qz", [P, 2, DC, 2, P])
            qf = sb("qf", [P, 2, DC, P])
            at = sb("at", [P, H0, P])
            state = sb("state", [P, DC, P])
            kvm = sb("kvm", [P, DC, P])
            fill = sb("fill", [P, BLOCKS0, 2])
            zero = sb("zero", [P, 4, D])
            ps_t = ps("ps_t", [P, 512])
            ps_qv = ps("ps_qv", [P, 512])
            ps_qT = ps("ps_qT", [P, 512])
            ps_a = ps("ps_a", [P, 4, 512])
            ps_o = ps("ps_o", [P, 512])
            names = ("turns mv_ready own_mv own_next consts x_first x weights const_ready fill_ready zero_ready filled own_dve kv_masked std_ready "
                     "xn_ready t_ready xnT_ready "
                     "qvps_ready sq_ready ss_ready rt_ready qv_ready qT_ready qz_ready a_ready at_ready "
                     "o_done state_ready xs_done").split()
            s = {n: sem(n) for n in names}
            ident, causal = self.const("ident"), self.const("causal")
            blocks, parity, keep = self.const("blocks"), self.const("parity"), self.const("keep")
            block = ctx.enter_context(nc.Block())

            @block.sync
            def _(sp):
                sp.dma_start(self.C[:], ins["consts"]).then_inc(s["consts"], 16)
                for part, name in ((slice(0, 4), "x_first"), (slice(4, NT), "x")):
                    sp.dma_start(x[:, part], ins["X"].rearrange("(n p) d -> p n d", p=P)[:, part]).then_inc(s[name], 16)
                for w, name in enumerate(("WqT", "WvT")):
                    sp.dma_start(wqv[:, :, w * D:(w + 1) * D],
                                 ins[name].rearrange("(c p) n -> p c n", p=P)).then_inc(s["weights"], 16)
                for w, name in enumerate(("qw", "vw")):
                    sp.dma_start(normw[:, w * D:(w + 1) * D],
                                 ins[name].partition_broadcast(P)).then_inc(s["weights"], 16)
                sp.wait_ge(s["fill_ready"], 2)
                sp.dma_start(self.table0[:].rearrange("(n p) w -> p n w", p=P), fill[:]).then_inc(s["filled"], 16)
                sp.dma_start(self.table1[:].rearrange("(n p) w -> p n w", p=P), fill[:, 0:E1 * CAP // P])\
                    .then_inc(s["filled"], 16)
                sp.wait_ge(s["zero_ready"], 1)
                for acc in (self.x_odd, self.out_odd):
                    for n in range(0, NT, 4):
                        sp.dma_start(acc[:].rearrange("(n p) d -> p n d", p=P)[:, n:n + 4], zero[:]).then_inc(s["filled"], 16)
                sp.wait_ge(s["filled"], 32 + 16 * 2 * NT // 4)

            @block.gpsimd
            def _(pool):
                pool.memset(self.eps[:, 0:1], LN_EPS).then_inc(s["const_ready"], 1)
                pool.memset(self.eps[:, 1:2], RMS_EPS).then_inc(s["const_ready"], 1)
                pool.memset(self.ones_bf[:], 1.0)
                pool.memset(fill[:].bitcast(U32)[:, :, 0], DROP).then_inc(s["fill_ready"], 1)
                pool.memset(fill[:, :, 1], 0.0).then_inc(s["fill_ready"], 1)
                pool.memset(zero[:], 0.0).then_inc(s["zero_ready"], 1)

            @block.vector
            def _(dve):
                link = Chain(dve, s["own_dve"])
                dve.memset(state[:], 0.0).then_inc(s["state_ready"], 1)
                dve.wait_ge(s["consts"], 16)
                dve.tensor_copy(self.tri[:], self.const("before"))
                own, tally = Chain(dve, s["own_mv"]), Chain(dve, s["own_next"])
                dve.wait_ge(s["x_first"], 16)

                def measure(i, r):
                    own.begin(i * 2)
                    own(dve.bn_stats(stats[:], x[:, bass.ds(i, 1), :].squeeze(1)))
                    stand_alone(dve, s["turns"])
                    dve.bn_aggr(mv[:, r % 4], stats[:]).then_inc(s["mv_ready"], 1)

                def tokens(i, r):
                    dve.wait_ge(s["std_ready"], i + 1)
                    own(dve.reciprocal(rstd[:, r % 4:r % 4 + 1], std[:, r % 4:r % 4 + 1]))
                    dve.tensor_scalar(xn[:, r % 4], x[:, bass.ds(i, 1), :].squeeze(1), mv[:, r % 4, 0:1],
                                      rstd[:, r % 4:r % 4 + 1], ALU.subtract, ALU.mult).then_inc(s["xn_ready"], 1)

                def measure_next(i):
                    dve.wait_ge(s["own_next"], i * 4 + 1)
                    tally.begin(i * 4 + 1)
                    stand_alone(dve, s["turns"])
                    tally(dve.bn_stats(stats[:], x[:, bass.ds(i, 1), :].squeeze(1)))
                    stand_alone(dve, s["turns"])
                    tally(dve.bn_aggr(agg[:], stats[:]))
                    tally(dve.tensor_copy(self.mv[:, bass.ds(i, 1), :].squeeze(1), agg[:]))

                def normalise(i, r):
                    link.begin(i * 2)
                    dve.wait_ge(s["sq_ready"], i + 1)
                    dve.tensor_reduce(ss[:], sq[:].rearrange("p (h d) -> p h d", d=D0), X, ALU.add)\
                        .then_inc(s["ss_ready"], 1)
                    dve.wait_ge(s["rt_ready"], i + 1)
                    link(dve.reciprocal(rr[:], rt[:]))
                    link(dve.tensor_tensor(qv1[:].rearrange("p (h d) -> p h d", d=D0),
                                           ps_qv[:].rearrange("p (h d) -> p h d", d=D0),
                                           rr[:].unsqueeze(2).broadcast_to([P, 2 * H0, D0]), ALU.mult))
                    dve.tensor_tensor(qv[:, r % 4], qv1[:], normw[:], ALU.mult).then_inc(s["qv_ready"], 1)

                def step(i, r):
                    if exists(i + 4, NT):
                        measure(i + 4, r)
                    atv = at[:].rearrange("p (c j r) l -> p j c r l", c=DC, j=4)
                    for j in range(4):
                        dve.wait_ge(s["a_ready"], i * 4 + (j + 1))
                        m = dve.tensor_tensor(atv[:, j], ps_a[:, j].rearrange("p (c r l) -> p c r l", c=DC, r=2),
                                              causal.unsqueeze(1).unsqueeze(1).broadcast_to([P, DC, 2, P]), ALU.mult)
                    m.then_inc(s["at_ready"], 1)
                    if exists(i + 2, NT):
                        normalise(i + 2, r + 2)
                    dve.wait_ge(s["o_done"], i + 1)
                    dve.scalar_tensor_tensor(kvm[:], ps_o[:, D:2 * D].rearrange("p (c e) -> p c e", c=DC),
                                             keep[:, bass.ds(i, 1)], blocks.unsqueeze(1).broadcast_to([P, DC, P]),
                                             ALU.mult, ALU.mult).then_inc(s["kv_masked"], 1)
                    dve.tensor_tensor(x[:, bass.ds(i, 1), :].squeeze(1), ps_o[:, 0:D],
                                      x[:, bass.ds(i, 1), :].squeeze(1), ALU.add).then_inc(s["own_next"], 1)
                    dve.wait_ge(s["kv_masked"], i + 1)
                    dve.scalar_tensor_tensor(state[:], state[:], keep[:, bass.ds(i, 1)], kvm[:],
                                             ALU.mult, ALU.add).then_inc(s["state_ready"], 1)
                    if exists(i + 4, NT):
                        tokens(i + 4, r)
                    measure_next(i)

                def prologue():
                    for i in range(4):
                        if i > 0:
                            dve.wait_ge(s["mv_ready"], i)
                        measure(i, i)
                        tokens(i, i)
                    dve.wait_ge(s["weights"], 64)
                    dve.wait_ge(s["x"], 16)
                    normalise(0, 0)
                    normalise(1, 1)
                pipeline(dve, NT, 4, prologue, step)

            @block.scalar
            def _(act):
                act.wait_ge(s["const_ready"], 2)

                def spread(i, r):
                    act.wait_ge(s["mv_ready"], i + 1)
                    act.activation(std[:, r % 4:r % 4 + 1], mv[:, r % 4, 1:2], ACT.Sqrt, bias=self.eps[:, 0:1])\
                        .then_inc(s["std_ready"], 1)

                def keys(i, r):
                    act.wait_ge(s["t_ready"], i + 1)
                    act.activation(xnT[:, r % 4], ps_t[:, 0:D], ACT.Copy).then_inc(s["xnT_ready"], 1)

                def squares(i):
                    act.wait_ge(s["qvps_ready"], i + 1)
                    act.activation(sq[:], ps_qv[:], ACT.Square).then_inc(s["sq_ready"], 1)

                def roots(i):
                    act.wait_ge(s["ss_ready"], i + 1)
                    act.activation(rt[:], ss[:], ACT.Sqrt, bias=self.eps[:, 1:2], scale=1.0 / D0)\
                        .then_inc(s["rt_ready"], 1)

                def queries(i, r):
                    act.wait_ge(s["qT_ready"], i + 1)
                    src = ps_qT[:, 0:D].rearrange("p (c l) -> p c l", c=DC)
                    act.activation(qz[:, r % 2, :, 0, :], src, ACT.Copy, scale=parity[:, 0:1])
                    act.activation(qz[:, r % 2, :, 1, :], src, ACT.Copy, scale=parity[:, 1:2])
                    act.activation(qf[:, r % 2], src, ACT.Copy).then_inc(s["qz_ready"], 1)

                def prologue():
                    for i in range(4):
                        spread(i, i)
                    for i in range(3):
                        keys(i, i)
                    for i in range(2):
                        squares(i)
                        roots(i)
                    queries(0, 0)

                def step(i, r):
                    if exists(i + 4, NT):
                        spread(i + 4, r)
                    if exists(i + 3, NT):
                        keys(i + 3, r + 3)
                    if exists(i + 2, NT):
                        squares(i + 2)
                    if exists(i + 1, NT):
                        queries(i + 1, r + 1)
                    if exists(i + 2, NT):
                        roots(i + 2)
                pipeline(act, NT, 4, prologue, step)

            @block.tensor
            def _(pe):
                pe.wait_ge(s["consts"], 16)
                pe.wait_ge(s["weights"], 64)

                def keys(i, r):
                    pe.wait_ge(s["xn_ready"], i + 1)
                    if not isinstance(i, int) or i > 0:
                        pe.wait_ge(s["xnT_ready"], i)
                    for c in range(DC):
                        m = pe.transpose(ps_t[:, c * P:(c + 1) * P], xn[:, r % 4, c * P:(c + 1) * P], ident)
                    m.then_inc(s["t_ready"], 1)

                def project(i, r):
                    pe.wait_ge(s["xnT_ready"], i + 1)
                    if not isinstance(i, int) or i > 0:
                        pe.wait_ge(s["qv_ready"], i)
                    for c in range(DC):
                        m = pe.matmul(ps_qv[:], xnT[:, r % 4, c * P:(c + 1) * P], wqv[:, c],
                                      start=c == 0, stop=c == DC - 1)
                    m.then_inc(s["qvps_ready"], 1)

                def queries(i, r):
                    pe.wait_ge(s["qv_ready"], i + 1)
                    for c in range(DC):
                        m = pe.transpose(ps_qT[:, c * P:(c + 1) * P], qv[:, r % 4, c * P:(c + 1) * P], ident)
                    m.then_inc(s["qT_ready"], 1)

                def step(i, r):
                    pe.wait_ge(s["qz_ready"], i + 1)
                    for j in range(4):
                        f = slice(32 * j, 32 * j + 32)
                        for c in range(DC):
                            m = pe.matmul(ps_a[:, j, c * D:(c + 1) * D], xnT[f, r, c * P:(c + 1) * P],
                                          qz[f, r % 2, c].rearrange("p r l -> p (r l)"), start=True, stop=True)
                        m.then_inc(s["a_ready"], 1)
                    if exists(i + 3, NT):
                        keys(i + 3, r + 3)
                    if exists(i + 2, NT):
                        project(i + 2, r + 2)
                    if exists(i + 1, NT):
                        queries(i + 1, r + 1)
                    pe.wait_ge(s["state_ready"], i + 1)
                    for c in range(DC):
                        pe.matmul(ps_o[:, D + c * P:D + (c + 1) * P], xn[:, r, c * P:(c + 1) * P],
                                  qv[:, r, D + c * P:D + (c + 1) * P], start=True, stop=True, skip_group_check=True)
                    for c in range(DC):
                        pe.matmul(ps_o[:, c * P:(c + 1) * P], qf[:, r % 2, c], state[:, c], start=c == 0, stop=False,
                                  skip_group_check=True)
                    pe.wait_ge(s["at_ready"], i + 1)
                    for h in range(H0):
                        m = pe.matmul(ps_o[:, h * D0:(h + 1) * D0], at[:, h, :], qv[:, r, D + h * D0:D + (h + 1) * D0],
                                      start=False, stop=h == H0 - 1, skip_group_check=True)
                    m.then_inc(s["o_done"], 1)

                def prologue():
                    for i in range(3):
                        keys(i, i)
                    for i in range(2):
                        project(i, i)
                    queries(0, 0)
                pipeline(pe, NT, 4, prologue, step)

    def route(self, moe, E, K, table, residual):
        nc, ins, x = self.nc, self.ins, self.x
        ctx, sb, ps, sem = self.scope(f"rt{moe}")
        SPAN = T if moe == 0 else CAP
        ROWS = BLOCKS0 * P if moe == 0 else E1 * CAP
        with ctx:
            std = sb("std", [P, NT])
            rstd = sb("rstd", [P, NT])
            xn = sb("xn", [P, 4, D])
            xnT = sb("xnT", [P, 2, D])
            wg = sb("wg", [P, DC, E])
            bg = sb("bg", [P, E])
            lg = sb("lg", [P, E])
            pr = sb("pr", [P, E])
            small = sb("small", [P, 4])
            top = sb("top", [P, 8])
            topi = sb("topi", [P, 8], U32)
            idx = sb("idx", [P, K])
            pos = sb("pos", [P, K])
            hot = sb("hot", [P, K, E])
            hotp = sb("hotp", [P, K, E])
            mask = sb("mask", [P, 2, E], BF16)
            seen = sb("seen", [P, E], BF16)
            slotf = sb("slotf", [P, K])
            over = sb("over", [P, K])
            wsum = sb("wsum", [P, 2])
            slot = sb("slot", [P, 4, K], U32)
            entry = sb("entry", [P, 4, K, 2])
            ps_t = ps("ps_t", [P, 512])
            ps_l = ps("ps_l", [P, 512])
            ps_p = ps("ps_p", [P, 512])
            if moe == 0:
                cnt, ntl, endt, off, onesf = (sb(n, [P, E]) for n in ("cnt", "ntl", "endt", "off", "onesf"))
                cnti = sb("cnti", [P, E], U32)
                below = sb("below", [1, ST0 + 1, E0])
                begin = sb("begin", [1, ST0 + 1, E0])
                texp, tbeg, live, blk = (sb(n, [1, ST0 + 1]) for n in ("texp", "tbeg", "live", "blk"))
                bsrc = sb("bsrc", [E0, 2 * F0 + D])
                brest = sb("brest", [E0, 2 * F0 + D])
                bpart = sb("bpart", [E0, 3, 2 * F0 + D], BF16)
            names = ("turns weights own std_ready xn_ready xn0_out xn1_out xn2_out xn3_out x_out t_ready "
                     "xnT_ready l_ready e_ready e_go mask_ready pos_ready cnt_ready w_go w_ready staged "
                     "scat0 scat1 scat2 scat3 experts_in bias_in bias_split bias_out").split()
            s = {n: sem(n) for n in names}
            ident, iota = self.const("ident"), self.const("iota")[:, 0:E]
            block = ctx.enter_context(nc.Block())
            PER = 10 if moe == 0 else 17
            mv = self.mv

            @block.sync
            def _(sp):
                sp.dma_start(wg[:], ins[f"router{moe}"].rearrange("(c p) n -> p c n", p=P)).then_inc(s["weights"], 16)
                if moe == 0:
                    sp.dma_start(bg[:], ins["bg"].partition_broadcast(P)).then_inc(s["weights"], 16)
                    sp.dma_start(bsrc[:, 0:2 * F0], ins["bgu"]).then_inc(s["bias_in"], 16)
                    sp.dma_start(bsrc[:, 2 * F0:], ins["bd"]).then_inc(s["bias_in"], 16)
                sp.dma_start(residual.rearrange("(n p) d -> p n d", p=P), x[:]).then_inc(s["x_out"], 16)
                if moe == 0:
                    for e in range(E0):
                        sp.dma_start(self.wgu0[:, e], ins["Wgu"][e].rearrange("(c p) n -> p c n", p=P))\
                                .then_inc(s["experts_in"], 16)
                        sp.dma_start(self.wd0[:, e], ins["Wd"][e].rearrange("(c p) n -> p c n", p=P))\
                                .then_inc(s["experts_in"], 16)
                rows = self.xn_dram[:].rearrange("(n p) d -> p n d", p=P)
                with sp.Fori(0, NT - 3, 4) as i:
                    for r in range(4):
                        sp.wait_ge(s["xn_ready"], i + (r + 1))
                        sp.dma_start(rows[:, bass.ds(i + r, 1), :].squeeze(1), xn[:, r]).then_inc(s[f"xn{r}_out"], 16)
                if moe == 0:
                    sp.wait_ge(s["bias_split"], 5)
                    for e in range(E0):
                        for k in range(3):
                            sp.dma_start(self.bias0[k:k + 1, e], bpart[e:e + 1, k]).then_inc(s["bias_out"], 16)
                    sp.wait_ge(s["bias_out"], 48 * E0)
                    sp.wait_ge(s["experts_in"], 32 * E0)
                sp.wait_ge(s["x_out"], 16)
                for r in range(4):
                    sp.wait_ge(s[f"xn{r}_out"], 4 * NT + 16)

            @block.vector
            def _(dve):
                link = Chain(dve, s["own"])
                dve.wait_ge(s["std_ready"], 1)
                link(dve.reciprocal(rstd[:], std[:]))
                dve.wait_ge(s["weights"], 32 if moe == 0 else 16)
                dve.memset(seen[:], 0.0)
                if moe == 0:
                    dve.wait_ge(s["bias_in"], 32)
                    part = Chain(dve, s["bias_split"])
                    part(dve.tensor_copy(bpart[:, 0], bsrc[:]))
                    part(dve.tensor_tensor(brest[:], bsrc[:], bpart[:, 0], ALU.subtract))
                    part(dve.tensor_copy(bpart[:, 1], brest[:]))
                    part(dve.tensor_tensor(bsrc[:], brest[:], bpart[:, 1], ALU.subtract))
                    part(dve.tensor_copy(bpart[:, 2], bsrc[:]))

                def tokens(i, r):
                    dve.wait_ge(s[f"xn{r % 4}_out"], i * 4 + (16 - 4 * (r % 4)))
                    dve.tensor_scalar(xn[:, r % 4], x[:, bass.ds(i, 1), :].squeeze(1), mv[:, bass.ds(i, 1), 0],
                                      rstd[:, bass.ds(i, 1)], ALU.subtract, ALU.mult).then_inc(s["xn_ready"], 1)

                def step(i, r):
                    link.begin(i * PER + 1)
                    if exists(i + 2, NT):
                        tokens(i + 2, r + 2)
                    dve.wait_ge(s["l_ready"], i + 1)
                    if moe == 0:
                        link(dve.tensor_tensor(lg[:], ps_l[:, 0:E], bg[:], ALU.add))
                        scores = lg
                    else:
                        link(dve.tensor_reduce(small[:, 0:1], ps_l[:, 0:E], X, ALU.max))
                        dve.tensor_scalar(small[:, 1:2], small[:, 0:1], -1.0, None, ALU.mult).then_inc(s["e_go"], 1)
                        dve.wait_ge(s["e_ready"], i + 1)
                        link(dve.tensor_reduce(small[:, 2:3], lg[:], X, ALU.add))
                        link(dve.reciprocal(small[:, 3:4], small[:, 2:3]))
                        link(dve.tensor_scalar(pr[:], lg[:], small[:, 3:4], None, ALU.mult))
                        scores = pr
                    stand_alone(dve, s["turns"])
                    link(dve.max(top[:], scores[:]))
                    if moe == 0:
                        if not isinstance(i, int) or i > 0:
                            dve.wait_ge(s["w_ready"], i)
                        dve.tensor_tensor(over[:, 0:1], top[:, 0:1], top[:, 1:2], ALU.subtract)
                        dve.tensor_tensor(over[:, 1:2], top[:, 1:2], top[:, 0:1], ALU.subtract).then_inc(s["w_go"], 1)
                    stand_alone(dve, s["turns"])
                    link(dve.max_index(topi[:], top[:], scores[:]))
                    link(dve.tensor_copy(idx[:], topi[:, 0:K]))
                    link(dve.tensor_tensor(hot[:], iota.unsqueeze(1).broadcast_to([P, K, E]),
                                           idx[:].unsqueeze(2).broadcast_to([P, K, E]), ALU.is_equal))
                    with nc.allow_low_precision(reason="sums of one-hot rows: 0 or 1"):
                        link(dve.tensor_reduce(mask[:, r % 2], hot[:].rearrange("p k e -> p e k"), X, ALU.add))
                    dve.sem_inc(s["mask_ready"], 1)
                    dve.wait_ge(s["pos_ready"], i + 1)
                    link(dve.tensor_tensor(seen[:], seen[:], mask[:, r % 2], ALU.add))
                    link(dve.tensor_tensor(hotp[:], hot[:],
                                           ps_p[:, 0:E].unsqueeze(1).broadcast_to([P, K, E]), ALU.mult))
                    link(dve.tensor_reduce(pos[:], hotp[:], X, ALU.add))
                    link(dve.scalar_tensor_tensor(slotf[:], idx[:], float(SPAN), pos[:], ALU.mult, ALU.add))
                    if moe == 1:
                        link(dve.tensor_scalar(over[:], pos[:], float(CAP), float(DROP), ALU.is_ge, ALU.mult))
                        link(dve.tensor_tensor(slotf[:], slotf[:], over[:], ALU.add))
                        link(dve.tensor_reduce(wsum[:, 0:1], top[:, 0:K], X, ALU.add))
                        link(dve.reciprocal(wsum[:, 1:2], wsum[:, 0:1]))
                    if not isinstance(i, int) or i >= 4:
                        dve.wait_ge(s[f"scat{r}"], i * (4 * K) - 4 * K * r)
                        stand_alone(dve, s["turns"])
                    dve.tensor_copy(slot[:, r], slotf[:])
                    if moe == 1:
                        dve.tensor_scalar(entry[:, r, :, 1], top[:, 0:K], wsum[:, 1:2], None, ALU.mult)
                    dve.tensor_copy(entry[:, r].bitcast(U32)[:, :, 0],
                                    self.const("token")[:, bass.ds(i, 1)].broadcast_to([P, K])).then_inc(s["staged"], 1)
                    dve.wait_ge(s["staged"], i + 1)
                    assert link.n == PER, link.n

                def prologue():
                    tokens(0, 0)
                    tokens(1, 1)
                pipeline(dve, NT, 4, prologue, step, peel_first=True)
                if moe == 0:
                    link.begin(1 + NT * PER)
                    dve.memset(onesf[:], 1.0)
                    dve.wait_ge(s["cnt_ready"], 1)
                    link(dve.tensor_scalar(cnt[:], ps_p[:, 0:E], float(P - 1), None, ALU.add))
                    link(dve.tensor_copy(cnti[:], cnt[:]))
                    link(dve.tensor_scalar(cnti[:], cnti[:], 7, None, ALU.logical_shift_right))
                    link(dve.tensor_copy(ntl[:], cnti[:]))
                    link(dve.tensor_tensor_scan(endt[:], onesf[:], ntl[:], 0.0, ALU.mult, ALU.add))
                    link(dve.tensor_tensor(off[:], endt[:], ntl[:], ALU.subtract))
                    every = [1, ST0 + 1, E]
                    tiles = self.const("tiles")[0:1]
                    link(dve.tensor_tensor(below[:], endt[0:1, :].unsqueeze(1).broadcast_to(every),
                                           tiles.unsqueeze(2).broadcast_to(every), ALU.is_le))
                    link(dve.tensor_reduce(texp[:], below[:], X, ALU.add))
                    link(dve.tensor_scalar(self.tile_expert[:, 0], texp[:], float(E - 1), None, ALU.min))
                    link(dve.tensor_tensor(begin[:], iota[0:1].unsqueeze(1).broadcast_to(every),
                                           texp[:].unsqueeze(2).broadcast_to(every), ALU.is_equal))
                    link(dve.tensor_tensor(begin[:], begin[:], off[0:1, :].unsqueeze(1).broadcast_to(every), ALU.mult))
                    link(dve.tensor_reduce(tbeg[:], begin[:], X, ALU.add))
                    link(dve.tensor_tensor(tbeg[:], tiles, tbeg[:], ALU.subtract))
                    link(dve.scalar_tensor_tensor(blk[:], texp[:], float(NT), tbeg[:], ALU.mult, ALU.add))
                    link(dve.tensor_scalar(live[:], texp[:], float(E), None, ALU.is_lt))
                    link(dve.tensor_scalar(blk[:], blk[:], float(1 - BLOCKS0), None, ALU.add))
                    link(dve.tensor_tensor(blk[:], blk[:], live[:], ALU.mult))
                    link(dve.tensor_scalar(self.tile_expert[:, 1], blk[:], float(BLOCKS0 - 1), None, ALU.add))

            @block.scalar
            def _(act):
                for r in range(4):
                    act.sem_inc(s[f"xn{r}_out"], 16)
                act.activation(std[:], mv[:, :, 1], ACT.Sqrt, bias=self.eps[:, 0:1]).then_inc(s["std_ready"], 1)

                def tokens(i, r):
                    act.wait_ge(s["t_ready"], i + 1)
                    act.activation(xnT[:, r % 2], ps_t[:, 0:D], ACT.Copy).then_inc(s["xnT_ready"], 1)

                def step(i, r):
                    if exists(i + 1, NT):
                        tokens(i + 1, r + 1)
                    if moe == 1:
                        act.wait_ge(s["e_go"], i + 1)
                        act.activation(lg[:], ps_l[:, 0:E], ACT.Exp, bias=small[:, 1:2]).then_inc(s["e_ready"], 1)
                    else:
                        act.wait_ge(s["w_go"], i + 1)
                        if not isinstance(i, int) or i >= 4:
                            act.wait_ge(s[f"scat{r}"], i * (4 * K) - 4 * K * r)
                        act.activation(entry[:, r, :, 1], over[:], ACT.Sigmoid).then_inc(s["w_ready"], 1)
                pipeline(act, NT, 4, lambda: tokens(0, 0), step, peel_first=True)

            @block.tensor
            def _(pe):
                pe.wait_ge(s["weights"], 32 if moe == 0 else 16)

                def tokens(i, r):
                    pe.wait_ge(s["xn_ready"], i + 1)
                    for c in range(DC):
                        m = pe.transpose(ps_t[:, c * P:(c + 1) * P], xn[:, r % 4, c * P:(c + 1) * P], ident)
                    m.then_inc(s["t_ready"], 1)

                def logits(i, r):
                    pe.wait_ge(s["xnT_ready"], i + 1)
                    for c in range(DC):
                        m = pe.matmul(ps_l[:, 0:E], xnT[:, r % 2, c * P:(c + 1) * P], wg[:, c], start=c == 0, stop=c == DC - 1)
                    m.then_inc(s["l_ready"], 1)

                def step(i, r):
                    logits(i, r)
                    if exists(i + 1, NT):
                        tokens(i + 1, r + 1)
                    pe.wait_ge(s["mask_ready"], i + 1)
                    pe.matmul(ps_p[:, 0:E], self.tri[:], mask[:, r % 2], start=True, stop=False)
                    pe.matmul(ps_p[:, 0:E], self.ones_bf[:], seen[:], start=False, stop=True).then_inc(s["pos_ready"], 1)
                pipeline(pe, NT, 4, lambda: tokens(0, 0), step)
                if moe == 0:
                    pe.wait_ge(s["own"], 1 + NT * PER)
                    pe.matmul(ps_p[:, 0:E], self.ones_bf[:], seen[:], start=True, stop=True).then_inc(s["cnt_ready"], 1)

            @block.gpsimd
            def _(pool):
                with pool.Fori(0, NT - 3, 4) as i:
                    for r in range(4):
                        pool.wait_ge(s["staged"], i + (r + 1))
                        stand_alone(pool, s["turns"])
                        if moe == 0:
                            pool.wait_ge(s["w_ready"], i + (r + 1))
                            stand_alone(pool, s["turns"])
                        for k in range(K):
                            pool.indirect_dma_start(table[:], bass.IndirectOffsetOnAxis(ap=slot[:, r, k:k + 1], axis=0),
                                                    entry[:, r, k, :], None, bounds_check=ROWS - 1, oob_is_err=False)\
                                .then_inc(s[f"scat{r}"], 16)
                for r in range(4):
                    pool.wait_ge(s[f"scat{r}"], 4 * K * NT)

    def experts(self, moe):
        nc, ins = self.nc, self.ins
        R, F, N = (P, F0, ST0 + 1) if moe == 0 else (CAP, F1, E1)
        FK = 128 if moe == 0 else 96
        targets = (self.x_acc[:], self.x_odd[:]) if moe == 0 else (self.out, self.out_odd[:])
        RING = 8
        AHEAD = 5
        WR = 8
        U = 8
        ctx, sb, ps, sem = self.scope(f"ex{moe}")
        with ctx:
            if moe == 0:
                ent = sb("ent", [R, RING, 2])
            else:
                ent = sb("ent", [R, N, 2])
            sid = sb("sid", [R, RING, 1], U32)
            wt = sb("wt", [R, RING])
            xg = sb("xg", [R, RING, D])
            xgT = sb("xgT", [P, 2, DC, R])
            gate = sb("gate", [R, F])
            sig = sb("sig", [R, 2, F])
            glu = sb("glu", [R, F])
            up = sb("up", [R, F])
            hid = sb("hid", [R, 2, F])
            hidT = sb("hidT", [FK, 2, R])
            y = sb("y", [R, 2, D])
            if moe == 1:
                wgu = sb("wgu", [P, WR, DC, 2 * F1])
                wd = sb("wd", [FK, WR, 2, D])
            ps_t = ps("ps_t", [P, 512])
            ps_g = ps("ps_g", [P, 2, 512])
            ps_h = ps("ps_h", [P, 512])
            ps_y = ps("ps_y", [P, 2, 512])
            names = ("turns cleared entries e0 e1 e2 e3 e4 e5 e6 e7 sid_ready g0 g1 g2 g3 g4 g5 g6 g7 t_ready xT_ready g_ready gate_ready "
                     "sig_ready hid_ready h_ready hT_ready y_ready ys_ready scat0 scat1 own w0 w1 w2 w3 w4 w5 w6 w7").split()
            s = {n: sem(n) for n in names}
            ident = self.const("ident")
            block = ctx.enter_context(nc.Block())
            LINKS = 2 if moe == 0 else 1

            @block.sync
            def _(sp):
                if moe == 0:
                    blocks = self.table0[:].rearrange("(n p) w -> p n w", p=P)

                    def entries(i, r):
                        b = sp.value_load(self.tile_expert[0:1, 1, bass.ds(i, 1)], min_val=0, max_val=BLOCKS0 - 1)
                        sp.dma_start(ent[:, r % RING], blocks[:, bass.ds(b, 1)].squeeze(1)).then_inc(s[f"e{r % RING}"], 16)

                    for i in range(RING):
                        entries(i, i)
                    with sp.Fori(0, N - 2 * RING + 1, RING) as j:
                        for r in range(RING):
                            sp.wait_ge(s["sid_ready"], j + (r + 1))
                            entries(j + (r + RING), r)
                else:
                    sp.dma_start(ent[:], self.table1[:].rearrange("(n r) w -> r n w", r=R)).then_inc(s["entries"], 16)

                    def weights(e, r):
                        sp.dma_start(wgu[:, r], ins["Wgu1"][bass.ds(e, 1)].squeeze(0)
                                     .rearrange("(c p) n -> p c n", p=P)).then_inc(s[f"w{r}"], 16)
                        sp.dma_start(wd[:, r], ins["Wd1"][bass.ds(e, 1)].squeeze(0)
                                     .rearrange("(c p) n -> p c n", p=FK)).then_inc(s[f"w{r}"], 16)
                    for r in range(WR):
                        weights(r, r)
                    with sp.Fori(0, N - 2 * WR + 1, WR) as j:
                        for r in range(WR):
                            sp.wait_ge(s["y_ready"], j + (r + 1))
                            weights(j + (r + WR), r)

            @block.gpsimd
            def _(pool):
                pool.memset(xg[:], 0.0).then_inc(s["cleared"], 1)
                pool.wait_ge(s["cleared"], 1)
                if moe == 1:
                    pool.wait_ge(s["entries"], 16)

                def gather(i, r):
                    r %= RING
                    if moe == 0:
                        pool.wait_ge(s[f"e{r}"], i * 2 + (16 - 2 * r))
                        stand_alone(pool, s["turns"])
                        src = ent[:, r:r + 1]
                    else:
                        src = ent[:, bass.ds(i, 1)]
                    pool.tensor_copy(wt[:, r:r + 1], src[:, :, 1])
                    pool.tensor_copy(sid[:, r], src.bitcast(U32)[:, :, 0]).then_inc(s["sid_ready"], 1)
                    pool.wait_ge(s["sid_ready"], i + 1)
                    stand_alone(pool, s["turns"])
                    pool.indirect_dma_start(xg[:, r], None, self.xn_dram[:],
                                            bass.IndirectOffsetOnAxis(ap=sid[:, r], axis=0),
                                            bounds_check=T - 1, oob_is_err=False).then_inc(s[f"g{r}"], 16)

                def step(i, r):
                    pool.wait_ge(s["ys_ready"], i + 1)
                    stand_alone(pool, s["turns"])
                    if not isinstance(i, int) or i > 1:
                        pool.wait_ge(s[f"scat{r % 2}"], i * 8 - 8 * (r % 2))
                        stand_alone(pool, s["turns"])
                    pool.indirect_dma_start(targets[r % 2], bass.IndirectOffsetOnAxis(ap=sid[:, r % RING], axis=0),
                                            y[:, r % 2], None, bounds_check=T - 1, oob_is_err=False,
                                            compute_op=ALU.add).then_inc(s[f"scat{r % 2}"], 16)
                    if exists(i + AHEAD, N):
                        gather(i + AHEAD, r + AHEAD)

                def prologue():
                    for i in range(AHEAD):
                        gather(i, i)
                pipeline(pool, N, U, prologue, step, peel_first=True)
                for q in range(2):
                    pool.wait_ge(s[f"scat{q}"], 8 * N)

            @block.tensor
            def _(pe):
                expert = {}

                def tokens(i, r):
                    at = r % RING
                    pe.wait_ge(s[f"g{at}"], i * 2 + (16 - 2 * at))
                    if not isinstance(i, int) or i > 0:
                        pe.wait_ge(s["xT_ready"], i)
                    stand_alone(pe, s["turns"])
                    for c in range(DC):
                        m = pe.transpose(ps_t[:, c * R:(c + 1) * R], xg[:, at, c * P:(c + 1) * P], ident[0:R, 0:R])
                    m.then_inc(s["t_ready"], 1)

                def expert_of(i):
                    if moe == 0:
                        return pe.value_load(self.tile_expert[0:1, 0, bass.ds(i, 1)], min_val=0, max_val=E0 - 1)

                def gate_up(i, r, e):
                    pe.wait_ge(s["xT_ready"], i + 1)
                    out = ps_g[0:R, r % 2, 0:2 * F]
                    if moe == 0:
                        stand_alone(pe, s["turns"])
                        pe.matmul(out, self.ones_bf[0:3, :], self.bias0[:, bass.ds(e, 1), 0:2 * F].squeeze(1),
                                  start=True, stop=False)
                        w = [self.wgu0[:, bass.ds(e, 1), c].squeeze(1) for c in range(DC)]
                    else:
                        pe.wait_ge(s[f"w{r % WR}"], i * 4 + (32 - 4 * (r % WR)))
                        w = [wgu[:, r % WR, c] for c in range(DC)]
                    for c in range(DC):
                        m = pe.matmul(out, xgT[:, r % 2, c], w[c], start=c == 0 and moe == 1, stop=c == DC - 1)
                    m.then_inc(s["g_ready"], 1)

                def step(i, r):
                    pe.wait_ge(s["hid_ready"], i + 1)
                    stand_alone(pe, s["turns"])
                    for c in range(2):
                        m = pe.transpose(ps_h[0:FK, c * R:(c + 1) * R], hid[:, r % 2, c * FK:(c + 1) * FK], ident[0:R, 0:R])
                    m.then_inc(s["h_ready"], 1)
                    if exists(i + 2, N):
                        tokens(i + 2, r + 2)
                    e = expert_of(i)
                    later = expert_of(i + 2) if exists(i + 2, N) else None
                    pe.wait_ge(s["hT_ready"], i + 1)
                    out = ps_y[0:R, r % 2, 0:D]
                    if moe == 0:
                        stand_alone(pe, s["turns"])
                        pe.matmul(out, self.ones_bf[0:3, :], self.bias0[:, bass.ds(e, 1), 2 * F:].squeeze(1),
                                  start=True, stop=False)
                        w = [self.wd0[:, bass.ds(e, 1), c].squeeze(1) for c in range(2)]
                    else:
                        w = [wd[:, r % WR, c] for c in range(2)]
                    for c in range(2):
                        m = pe.matmul(out, hidT[:, c], w[c], start=c == 0 and moe == 1, stop=c == 1)
                    m.then_inc(s["y_ready"], 1)
                    if exists(i + 2, N):
                        gate_up(i + 2, r + 2, later)

                def prologue():
                    for i in range(2):
                        tokens(i, i)
                    for i in range(2):
                        gate_up(i, i, expert_of(i))
                pipeline(pe, N, U, prologue, step)

            @block.scalar
            def _(act):
                def tokens(i, r):
                    act.wait_ge(s["t_ready"], i + 1)
                    act.activation(xgT[:, r % 2], ps_t[:, 0:DC * R].rearrange("p (c r) -> p c r", c=DC), ACT.Copy)\
                        .then_inc(s["xT_ready"], 1)

                def sigmoid(i, r):
                    if moe == 0:
                        act.wait_ge(s["gate_ready"], i + 1)
                        act.activation(sig[:, r % 2], gate[:], ACT.Sigmoid, scale=1.702).then_inc(s["sig_ready"], 1)
                    else:
                        act.wait_ge(s["g_ready"], i + 1)
                        act.activation(sig[:, r % 2], ps_g[0:R, r % 2, 0:F], ACT.Sigmoid).then_inc(s["sig_ready"], 1)

                def step(i, r):
                    if exists(i + 1, N):
                        sigmoid(i + 1, r + 1)
                    act.wait_ge(s["h_ready"], i + 1)
                    act.activation(hidT[:], ps_h[0:FK, 0:2 * R].rearrange("p (c r) -> p c r", c=2), ACT.Copy)\
                        .then_inc(s["hT_ready"], 1)
                    if exists(i + 2, N):
                        tokens(i + 2, r + 2)

                def prologue():
                    tokens(0, 0)
                    tokens(1, 1)
                    sigmoid(0, 0)
                pipeline(act, N, U, prologue, step)

            @block.vector
            def _(dve):
                link = Chain(dve, s["own"])

                def activate(i, r):
                    link.begin(i * LINKS)
                    dve.wait_ge(s["g_ready"], i + 1)
                    if not isinstance(i, int) or i > 0:
                        dve.wait_ge(s["hid_ready"], i)
                    g, u = ps_g[0:R, r % 2, 0:F], ps_g[0:R, r % 2, F:2 * F]
                    if moe == 0:
                        dve.tensor_scalar(gate[:], g, 7.0, None, ALU.min).then_inc(s["gate_ready"], 1)
                        link(dve.tensor_scalar(up[:], u, 7.0, -7.0, ALU.min, ALU.max))
                        dve.wait_ge(s["sig_ready"], i + 1)
                        link(dve.tensor_tensor(glu[:], gate[:], sig[:, r % 2], ALU.mult))
                        dve.scalar_tensor_tensor(hid[:, r % 2], up[:], 1.0, glu[:], ALU.add, ALU.mult)\
                            .then_inc(s["hid_ready"], 1)
                    else:
                        dve.wait_ge(s["sig_ready"], i + 1)
                        link(dve.tensor_tensor(glu[:], g, sig[:, r % 2], ALU.mult))
                        dve.tensor_tensor(hid[:, r % 2], u, glu[:], ALU.mult).then_inc(s["hid_ready"], 1)

                def step(i, r):
                    if exists(i + 1, N):
                        activate(i + 1, r + 1)
                    dve.wait_ge(s["y_ready"], i + 1)
                    if not isinstance(i, int) or i >= 2:
                        dve.wait_ge(s[f"scat{r % 2}"], i * 8 - 8 * (r % 2))
                    dve.tensor_scalar(y[:, r % 2], ps_y[0:R, r % 2, 0:D], wt[:, r % RING:r % RING + 1], None, ALU.mult)\
                        .then_inc(s["ys_ready"], 1)
                pipeline(dve, N, U, lambda: activate(0, 0), step, peel_first=True)

    def project(self):
        nc, ins = self.nc, self.ins
        ctx, sb, ps, sem = self.scope("pj")
        W = H * DH
        with ctx:
            x = sb("x", [P, NT, D])
            wdown = sb("wdown", [P, DC, 2, P])
            wup = sb("wup", [P, 3, W])
            lnw = sb("lnw", [P, DC, 2])
            rope = sb("rope", [P, TB, 2, DH])
            xo = sb("xo", [P, NT, D])
            stats = sb("stats", [P, 6])
            mv = sb("mv", [P, 2, 4, 2])
            std = sb("std", [P, 2, 4])
            rstd = sb("rstd", [P, 2, 4])
            xn = sb("xn", [P, 4, D])
            hn = sb("hn", [P, 4, D])
            hT = sb("hT", [P, 2, DC, P])
            cT = sb("cT", [P, 2, 2, P])
            t1 = sb("t1", [P, 2, W])
            t2 = sb("t2", [P, 2, W])
            qkv = sb("qkv", [P, 2, 3, W])
            ps_t = ps("ps_t", [P, 512])
            ps_c = ps("ps_c", [P, 512])
            ps_u = ps("ps_u", [P, 3, W])
            names = ("turns mv1_ready mv2_ready x0 x1 x2 x3 x_sum x_out weights own std1_ready std2_ready hn_ready "
                     "t_ready hT_ready c_ready cT_ready q_ready k_ready v_ready q_rot v_copied t_made q0_out q1_out").split()
            s = {n: sem(n) for n in names}
            ident = self.const("ident")
            block = ctx.enter_context(nc.Block())

            @block.sync
            def _(sp):
                for q in range(4):
                    part = slice(q * NT // 4, (q + 1) * NT // 4)
                    for dst, src in ((x, self.x_acc), (xo, self.x_odd)):
                        sp.dma_start(dst[:, part], src[:].rearrange("(n p) d -> p n d", p=P)[:, part])\
                            .then_inc(s[f"x{q}"], 16)
                for w, name in enumerate(("w_down_qT", "w_down_kvT")):
                    sp.dma_start(wdown[:, :, w], ins[name].rearrange("(c p) n -> p c n", p=P)).then_inc(s["weights"], 16)
                for w, name in enumerate(("w_up_qT", "w_up_kT", "w_up_vT")):
                    sp.dma_start(wup[:, w], ins[name]).then_inc(s["weights"], 16)
                sp.dma_start(lnw[:], ins["ln"]).then_inc(s["weights"], 16)
                sp.dma_start(rope[:], ins["rope"].rearrange("p n (w d) -> p n w d", w=2)).then_inc(s["weights"], 16)
                acc = self.x_acc[:].rearrange("(n p) d -> p n d", p=P)
                for bt in range(B):
                    g0 = bt * (H // 2)
                    dst = self.qkv[g0:g0 + H // 2].rearrange("g (n p) w c -> w p n g c", p=P)
                    with sp.Fori(0, TB - 1, 2) as j:
                        sp.wait_ge(s["x_sum"], j + (bt * TB + 2))
                        sp.dma_start(acc[:, bass.ds(j + bt * TB, 2)], x[:, bass.ds(j + bt * TB, 2)]).then_inc(s["x_out"], 16)
                        for p in range(2):
                            sp.wait_ge(s["q_rot"], j * 2 + (2 * bt * TB + 2 * p + 4))
                            stand_alone(sp, s["turns"])
                            sp.wait_ge(s["v_copied"], j + (bt * TB + p + 2))
                            stand_alone(sp, s["turns"])
                            for w in range(3):
                                sp.dma_start(dst[w][:, bass.ds(j + p, 1)].squeeze(1),
                                             qkv[:, p, w].rearrange("p (g c) -> p g c", c=P))\
                                    .then_inc(s[f"q{p}_out"], 16)
                sp.wait_ge(s["x_out"], 8 * NT)
                sp.wait_ge(s["q0_out"], 24 * NT + 48)
                sp.wait_ge(s["q1_out"], 24 * NT + 48)

            @block.vector
            def _(dve):
                link = Chain(dve, s["own"])
                LINKS, FIRST = 6, 4 * 2 + 3 * 3 + 2 * 1

                def rows(i):
                    return bass.ds(i, 1)

                def statistics(src, w, r, ready):
                    link(dve.bn_stats(stats[:], src))
                    stand_alone(dve, s["turns"])
                    dve.bn_aggr(mv[:, w, r % 4], stats[:]).then_inc(s[ready], 1)

                def total(i, r):
                    link(dve.tensor_tensor(x[:, rows(i)].squeeze(1), x[:, rows(i)].squeeze(1),
                                           xo[:, rows(i)].squeeze(1), ALU.add))
                    stand_alone(dve, s["turns"])
                    if not isinstance(i, int) or i > 3:
                        dve.wait_ge(s["mv2_ready"], i)
                        stand_alone(dve, s["turns"])
                    elif i > 0:
                        dve.wait_ge(s["mv1_ready"], i)
                    statistics(x[:, rows(i)].squeeze(1), 0, r, "mv1_ready")

                def normalised(i, r):
                    dve.wait_ge(s["std1_ready"], i + 1)
                    link(dve.reciprocal(rstd[:, 0, r % 4:r % 4 + 1], std[:, 0, r % 4:r % 4 + 1]))
                    if not isinstance(i, int) or i > 0:
                        dve.wait_ge(s["x_sum"], i)
                    link(dve.tensor_scalar(xn[:, r % 4], x[:, rows(i)].squeeze(1), mv[:, 0, r % 4, 0:1],
                                           rstd[:, 0, r % 4:r % 4 + 1], ALU.subtract, ALU.mult))
                    dve.wait_ge(s["mv1_ready"], i + 1 if not isinstance(i, int) or i >= 3 else 4)
                    if not isinstance(i, int) or i > 0:
                        stand_alone(dve, s["turns"])
                        dve.wait_ge(s["mv2_ready"], i)
                    stand_alone(dve, s["turns"])
                    statistics(xn[:, r % 4], 1, r, "mv2_ready")
                    dve.tensor_tensor(x[:, rows(i)].squeeze(1), x[:, rows(i)].squeeze(1), xn[:, r % 4], ALU.add)\
                        .then_inc(s["x_sum"], 1)

                def tokens(i, r):
                    dve.wait_ge(s["std2_ready"], i + 1)
                    link(dve.reciprocal(rstd[:, 1, r % 4:r % 4 + 1], std[:, 1, r % 4:r % 4 + 1]))
                    dve.tensor_scalar(hn[:, r % 4], xn[:, r % 4], mv[:, 1, r % 4, 0:1],
                                      rstd[:, 1, r % 4:r % 4 + 1], ALU.subtract, ALU.mult).then_inc(s["hn_ready"], 1)

                def ahead(i, r):
                    if not isinstance(i, int) or i <= NT - 4:
                        link.begin(i * LINKS + FIRST)
                    if exists(i + 2, NT):
                        tokens(i + 2, r + 2)
                    if exists(i + 3, NT):
                        normalised(i + 3, r + 3)
                    if exists(i + 4, NT):
                        total(i + 4, r + 4)

                def back(i, b, p):
                    for w, ready in enumerate(("q_ready", "k_ready")):
                        dve.wait_ge(s[ready], i + 1)
                        dve.wait_ge(s["q_rot"], i * 2 + (w + 1))
                        src = ps_u[:, w].rearrange("p (h e r) -> p h e r", h=H, e=2)
                        cs = rope[:, bass.ds(b, 1), 0, :].broadcast_to([P, H, DH]).rearrange("p h (e r) -> p h e r", e=2)
                        sn = rope[:, bass.ds(b, 1), 1, :].broadcast_to([P, H, DH]).rearrange("p h (e r) -> p h e r", e=2)
                        a = t1[:, w].rearrange("p (h e r) -> p h e r", h=H, e=2)
                        c = t2[:, w].rearrange("p (h e r) -> p h e r", h=H, e=2)
                        dve.tensor_tensor(a, src, cs, ALU.mult)
                        dve.tensor_tensor(c[:, :, 0], src[:, :, 1], sn[:, :, 0], ALU.mult)
                        dve.tensor_tensor(c[:, :, 1], src[:, :, 0], sn[:, :, 1], ALU.mult).then_inc(s["t_made"], 1)

                for q in range(4):
                    dve.wait_ge(s[f"x{q}"], 32)
                link.begin(0)
                for i in range(4):
                    total(i, i)
                for i in range(3):
                    normalised(i, i)
                for i in range(2):
                    tokens(i, i)
                dve.wait_ge(s["weights"], 16 * 7)
                for bt in range(B):
                    base = bt * TB
                    last = TB - (4 if bt == B - 1 else 0)
                    with dve.Fori(0, last - 3, 4) as j:
                        for r in range(4):
                            ahead(j + (base + r), r)
                            back(j + (base + r), j + r, r % 2)
                    for r in range(last, TB):
                        ahead(base + r, r)
                        back(base + r, r, r % 2)

            @block.gpsimd
            def _(pool):
                pool.sem_inc(s["q_rot"], 2)
                with pool.Fori(0, NT - 1, 2) as j:
                    for p in range(2):
                        pool.wait_ge(s[f"q{p}_out"], j * 24 + 48)
                        stand_alone(pool, s["turns"])
                        for w in range(2):
                            pool.wait_ge(s["t_made"], j * 2 + (2 * p + w + 3))
                            stand_alone(pool, s["turns"])
                            pool.tensor_tensor(qkv[:, p, w], t1[:, w], t2[:, w], ALU.add).then_inc(s["q_rot"], 1)

            @block.scalar
            def _(act):
                act.sem_inc(s["q0_out"], 48)
                act.sem_inc(s["q1_out"], 48)
                def root(i, r, w):
                    act.wait_ge(s[f"mv{w + 1}_ready"], i + 1)
                    act.activation(std[:, w, r % 4:r % 4 + 1], mv[:, w, r % 4, 1:2], ACT.Sqrt, bias=self.eps[:, 0:1])\
                        .then_inc(s[f"std{w + 1}_ready"], 1)

                def tokens(i, r):
                    act.wait_ge(s["t_ready"], i + 1)
                    for c in range(DC):
                        m = act.activation(hT[:, r % 2, c], ps_t[:, c * P:(c + 1) * P], ACT.Identity,
                                           bias=lnw[:, c, 1:2], scale=lnw[:, c, 0:1])
                    m.then_inc(s["hT_ready"], 1)

                def down(i, r):
                    act.wait_ge(s["c_ready"], i + 1)
                    act.activation(cT[:, r % 2], ps_c[:, 0:2 * P].rearrange("p (w l) -> p w l", w=2), ACT.Copy)\
                        .then_inc(s["cT_ready"], 1)

                def step(i, r):
                    if exists(i + 2, NT):
                        tokens(i + 2, r + 2)
                    if exists(i + 1, NT):
                        down(i + 1, r + 1)
                    p = r % 2
                    act.wait_ge(s["v_ready"], i + 1)
                    act.wait_ge(s[f"q{p}_out"], i * 24 + (48 if p == 0 else 24))
                    act.activation(qkv[:, p, 2], ps_u[:, 2], ACT.Copy).then_inc(s["v_copied"], 1)
                    if exists(i + 3, NT):
                        root(i + 3, r + 3, 1)
                    if exists(i + 4, NT):
                        root(i + 4, r + 4, 0)

                def prologue():
                    for i in range(4):
                        root(i, i, 0)
                    for i in range(3):
                        root(i, i, 1)
                    act.wait_ge(s["weights"], 16 * 7)
                    tokens(0, 0)
                    tokens(1, 1)
                    down(0, 0)
                pipeline(act, NT, 4, prologue, step)

            @block.tensor
            def _(pe):
                pe.sem_inc(s["t_made"], 2)
                pe.sem_inc(s["v_copied"], 1)
                pe.wait_ge(s["weights"], 16 * 7)

                def tokens(i, r):
                    pe.wait_ge(s["hn_ready"], i + 1)
                    if not isinstance(i, int) or i > 0:
                        pe.wait_ge(s["hT_ready"], i)
                    for c in range(DC):
                        m = pe.transpose(ps_t[:, c * P:(c + 1) * P], hn[:, r % 4, c * P:(c + 1) * P], ident)
                    m.then_inc(s["t_ready"], 1)

                def down(i, r):
                    pe.wait_ge(s["hT_ready"], i + 1)
                    for w in range(2):
                        for c in range(DC):
                            m = pe.matmul(ps_c[:, w * P:(w + 1) * P], wdown[:, c, w], hT[:, r % 2, c],
                                          start=c == 0, stop=c == DC - 1)
                    m.then_inc(s["c_ready"], 1)

                def step(i, r):
                    pe.wait_ge(s["cT_ready"], i + 1)
                    if exists(i + 2, NT):
                        tokens(i + 2, r + 2)
                    if exists(i + 1, NT):
                        down(i + 1, r + 1)
                    for w, (ready, src, free, value) in enumerate((
                            ("q_ready", 0, "t_made", i * 2 + 1), ("k_ready", 1, "t_made", i * 2 + 2),
                            ("v_ready", 1, "v_copied", i + 1))):
                        pe.wait_ge(s[free], value)
                        for h in range(W // 512):
                            m = pe.matmul(ps_u[:, w, h * 512:(h + 1) * 512], cT[:, r % 2, src],
                                          wup[:, w, h * 512:(h + 1) * 512], start=True, stop=True)
                        m.then_inc(s[ready], 1)

                def prologue():
                    tokens(0, 0)
                    tokens(1, 1)
                    down(0, 0)
                pipeline(pe, NT, 4, prologue, step)

    def softmax_attention(self):
        nc = self.nc
        NG = NQB
        NU = (L // P) * (L // QB)
        items = [("K", g) for g in range(NG)] + [("Q", g) for g in range(NG)]
        for u in range(NU):
            items.append(("U", u))
            if u % 16 == 4 and u > 16:
                items.append(("M", u // 16 - 1))
        items.append(("M", NG - 1))
        NI = len(items)
        SLOTS = NQB * KC // 2
        plan = [items[2 * n:2 * n + 2] for n in range(4)] + [items[8 + 3 * n:min(11 + 3 * n, NI - 1)] for n in range(23)]
        plan += [[], [], items[NI - 1:], [], []]
        assert len(plan) == SLOTS and sum(plan, []) == items and NI % 2 == 0
        SHARED = [t for t in range(SLOTS - 4) if t < 7 or t % 2 or t > 18]
        HEADS = B * H
        MROW, MROW2 = DH, DH + 32
        ctx, sb, ps, sem = self.scope("at")
        with ctx:
            kd = sb("kd", [P, 2, KC, 2, DH])
            qd = sb("qd", [P, 2, KC, 2, DH])
            vf = sb("vf", [P, 2, KC, DH])
            vh = sb("vh", [P, 2, KC, P], F32R)
            vl = sb("vl", [P, 2, KC, P], F32R)
            k1 = [sb(f"k1_{i}", [P, L], F32R) for i in range(2)]
            k2 = [sb(f"k2_{i}", [P, L], F32R) for i in range(2)]
            q1 = [sb(f"q1_{i}", [P, L], F32R) for i in range(2)]
            q2 = [sb(f"q2_{i}", [P, L], F32R) for i in range(2)]
            mx = sb("mx", [P, NU])
            mg = sb("mg", [P, KC])
            nm = sb("nm", [P, KC])
            NP = 4
            pf = sb("pf", [P, NP, 2 * QB])
            ph = sb("ph", [P, NP, 2 * QB], F32R)
            pl = sb("pl", [P, NP, 2 * QB], F32R)
            o_st = sb("o_st", [DH + 1, 2, QB])
            ps_s = ps("ps_s", [P, 2, 2 * QB])
            ps_v = ps("ps_v", [P, 2, QB])
            ps_r = ps("ps_r", [P, 2, QB])
            names = ("turns kd0 kd1 qd0 qd1 v0 v1 fixed ring_full ring_free own k1_ready k_copied q1_ready nm_ready "
                     "q2_ready s_full p_ready pl_ready pl2_ready vh_ready v_split pv_done o_ready o0_out o1_out").split()
            s = {n: sem(n) for n in names}
            ident = self.const("ident")
            block = ctx.enter_context(nc.Block())

            @block.sync
            def _(sp):
                def load_qk(pr, hh):
                    for d, name, w in ((kd, "kd", 1), (qd, "qd", 0)):
                        src = self.qkv[bass.ds(pr, 1), :, w, hh * DH:(hh + 1) * DH].squeeze(0)\
                            .rearrange("(n p) c -> p n c", p=P)
                        for twice in range(2):
                            sp.dma_start(d[:, hh, :, twice, :], src).then_inc(s[f"{name}{hh}"], 16)

                def load_v(pr, hh):
                    src = self.qkv[bass.ds(pr, 1), :, 2, hh * DH:(hh + 1) * DH].squeeze(0)\
                        .rearrange("(n p) c -> p n c", p=P)
                    sp.dma_start(vf[:, hh], src).then_inc(s[f"v{hh}"], 16)

                def store_o(pr, hh):
                    for qb in range(NQB):
                        sp.wait_ge(s["o_ready"], pr * (2 * NQB) + (hh * NQB + qb + 3))
                        sp.dma_start(self.o_dram[bass.ds(pr, 1), hh * DH:(hh + 1) * DH, qb * QB:(qb + 1) * QB].squeeze(0),
                                     o_st[0:DH, qb % 2]).then_inc(s[f"o{qb % 2}_out"], 16)
                        sp.dma_start(self.den[bass.ds(pr, 1), hh, qb * QB:(qb + 1) * QB],
                                     o_st[DH:DH + 1, qb % 2]).then_inc(s[f"o{qb % 2}_out"], 16)

                load_qk(0, 0)
                load_qk(0, 1)
                load_v(0, 0)
                load_v(0, 1)
                with sp.Fori(0, PAIRS - 1) as pr:
                    for hh in range(2):
                        sp.wait_ge(s["ring_full"], pr * (2 * NI) + (hh * NI + 8))
                        load_qk(pr + 1, hh)
                        sp.wait_ge(s["v_split"], pr * 2 + (hh + 1))
                        load_v(pr + 1, hh)
                        store_o(pr, hh)
                for hh in range(2):
                    store_o(PAIRS - 1, hh)
                for ob in range(2):
                    sp.wait_ge(s[f"o{ob}_out"], 32 + 32 * HEADS * NQB // 2)

            @block.gpsimd
            def _(pool):
                link = Chain(pool, s["fixed"])
                link(pool.memset(vh[:, :, :, DH:].bitcast(F32), 1.0))
                link(pool.memset(vl[:, :, :, DH:].bitcast(F32), 0.0))
                for i in range(2):
                    link(pool.memset(k2[i][DH:P, :].bitcast(F32), 0.0))
                    link(pool.memset(q2[i][DH:P, :].bitcast(F32), 0.0))
                    for r in (MROW, MROW2):
                        link(pool.memset(k2[i][r:r + 1, :].bitcast(F32), 1.0))

                def split_values(g, hh, half):
                    pool.wait_ge(s[f"v{hh}"], half * 16 + 16)
                    stand_alone(pool, s["turns"])
                    if not isinstance(g, int) or g > 0:
                        pool.wait_ge(s["pv_done"], g * SLOTS + (NP - SLOTS))
                        stand_alone(pool, s["turns"])
                    pool.tensor_copy(vh[:, hh, :, 0:DH], vf[:, hh]).then_inc(s["vh_ready"], 1)

                def low_values(g, hh):
                    pool.wait_ge(s["vh_ready"], g + 1)
                    stand_alone(pool, s["turns"])
                    pool.tensor_tensor(vl[:, hh, :, 0:DH], vf[:, hh], vh[:, hh, :, 0:DH].bitcast(F32), ALU.subtract)\
                        .then_inc(s["v_split"], 1)

                def keys(g, hh, n):
                    at = slice(n * QB, (n + 1) * QB)
                    pool.wait_ge(s["k1_ready"], g * NG + (n + 1))
                    stand_alone(pool, s["turns"])
                    pool.tensor_copy(k2[hh][0:DH, at], k1[hh][0:DH, at]).then_inc(s["k_copied"], 1)

                def low_part(g, n):
                    if n % SLOTS not in SHARED:
                        return
                    pool.wait_ge(s["p_ready"], g * SLOTS + (n + 3))
                    stand_alone(pool, s["turns"])
                    at = slice(QB, 2 * QB)
                    pool.tensor_tensor(pl[:, n % NP, at], pf[:, n % NP, at], ph[:, n % NP, at].bitcast(F32),
                                       ALU.subtract).then_inc(s["pl2_ready"], 1)

                def head(pr, hh, prepare):
                    g, nxt = pr * 2 + hh, pr * 2 + (hh + 1)
                    for n in range(SLOTS):
                        if n + 1 < SLOTS or prepare:
                            low_part(g, n + 1)
                        if prepare and n == 7:
                            split_values(nxt, 1 - hh, pr + hh)
                        elif prepare and n == 9:
                            low_values(nxt, 1 - hh)
                        elif prepare and n in (11, 13, 15, 17):
                            keys(nxt, 1 - hh, (n - 11) // 2)

                split_values(0, 0, 0)
                low_values(0, 0)
                for n in range(NG):
                    keys(0, 0, n)
                low_part(0, 0)
                with pool.Fori(0, PAIRS - 1) as pr:
                    head(pr, 0, True)
                    head(pr, 1, True)
                head(PAIRS - 1, 0, True)
                head(PAIRS - 1, 1, False)

            @block.vector
            def _(dve):
                link = Chain(dve, s["own"])
                LH = 2 * NG + 2 * NG + NG + NG
                dve.sem_inc(s["ring_free"], 2)
                dve.wait_ge(s["fixed"], 10)
                count = {"c": 0}

                def item(pr, hh, kind, n, index, base):
                    dve.wait_ge(s["ring_full"], base * NI + (index + 1))
                    bank = ps_r[:, index % 2]
                    at = slice(n * QB, (n + 1) * QB)
                    if kind == "K":
                        dve.tensor_copy(k1[hh][:, at], bank).then_inc(s["k1_ready"], 1)
                        dve.wait_ge(s["k1_ready"], base * NG + (n + 1))
                        low = k1[hh][DH:P, at]
                        dve.tensor_tensor(low, bank[DH:P], low.bitcast(F32), ALU.subtract).then_inc(s["ring_free"], 1)
                    elif kind == "Q":
                        dve.tensor_copy(q1[hh][:, at], bank).then_inc(s["q1_ready"], 1)
                        dve.wait_ge(s["q1_ready"], base * NG + (n + 1))
                        dve.tensor_tensor(q2[hh][0:DH, at], bank[0:DH], q1[hh][0:DH, at].bitcast(F32), ALU.subtract)\
                            .then_inc(s["ring_free"], 1)
                    elif kind == "U":
                        dve.tensor_reduce(mx[:, n:n + 1], bank, X, ALU.max).then_inc(s["ring_free"], 1)
                        if n % 16 == 15:
                            g = n // 16
                            dve.wait_ge(s["ring_free"], base * NI + (index + 3))
                            mxv = mx[:, n - 15:n + 1].rearrange("p (t k) -> p t k", k=4)
                            own(base, dve.tensor_reduce(mg[:, 4 * g:4 * g + 4], mxv, X, ALU.max))
                            dve.tensor_scalar(nm[:, 4 * g:4 * g + 4], mg[:, 4 * g:4 * g + 4], -1.0, None, ALU.mult)\
                                .then_inc(s["nm_ready"], 1)
                    else:
                        own(base, dve.tensor_copy(q2[hh][MROW:MROW + 1, at], bank[0:1]))
                        dve.tensor_tensor(q2[hh][MROW2:MROW2 + 1, at], bank[0:1],
                                          q2[hh][MROW:MROW + 1, at].bitcast(F32), ALU.subtract)\
                            .then_inc(s["ring_free"], 1)
                        dve.wait_ge(s["ring_free"], base * NI + (index + 3))
                        dve.sem_inc(s["q2_ready"], 1)

                def own(base, ins_):
                    count["c"] += 1
                    ins_.then_inc(s["own"], 1)
                    dve.wait_ge(s["own"], base * (2 * NG) + count["c"])

                def low_part(g, n):
                    dve.wait_ge(s["p_ready"], g * SLOTS + (n + 3))
                    at = slice(0, QB if n % SLOTS in SHARED else 2 * QB)
                    dve.tensor_tensor(pl[:, n % NP, at], pf[:, n % NP, at], ph[:, n % NP, at].bitcast(F32), ALU.subtract)\
                        .then_inc(s["pl_ready"], 1)

                def head(pr, hh, prepare):
                    g = pr * 2 + hh
                    nxt = pr * 2 + (hh + 1)
                    count["c"] = 0
                    index = 0
                    for n in range(SLOTS):
                        work = list(plan[n]) if prepare else []
                        for place in range(3):
                            if place == 0 and (n + 1 < SLOTS or prepare):
                                low_part(g, n + 1)
                            if work:
                                item(pr, 1 - hh, *work.pop(0), index, nxt)
                                index += 1

                for index, (kind, m) in enumerate(items):
                    item(0, 0, kind, m, index, 0)
                low_part(0, 0)
                with dve.Fori(0, PAIRS - 1) as pr:
                    head(pr, 0, True)
                    head(pr, 1, True)
                head(PAIRS - 1, 0, True)
                head(PAIRS - 1, 1, False)

            @block.scalar
            def _(act):
                act.sem_inc(s["pv_done"], NP)
                act.sem_inc(s["p_ready"], 2)
                act.sem_inc(s["o_ready"], 2)
                act.sem_inc(s["o0_out"], 32)
                act.sem_inc(s["o1_out"], 32)

                def output(g, qb):
                    act.wait_ge(s["pv_done"], g * SLOTS + ((qb + 1) * 8 + NP))
                    act.wait_ge(s[f"o{qb % 2}_out"], g * 64 + (32 * (qb // 2) + 32))
                    act.activation(o_st[:, qb % 2], ps_v[0:DH + 1, qb % 2], ACT.Copy).then_inc(s["o_ready"], 1)

                def pair(pr):
                    for n in range(2 * SLOTS):
                        act.wait_ge(s["s_full"], pr * (2 * SLOTS) + (n + 1))
                        act.wait_ge(s["pv_done"], pr * (2 * SLOTS) + (n + 1))
                        act.activation(pf[:, n % NP], ps_s[:, n % 2], ACT.Exp, scale=DH ** -0.5)
                        act.activation(ph[:, n % NP], ps_s[:, n % 2], ACT.Exp, scale=DH ** -0.5)\
                            .then_inc(s["p_ready"], 1)
                        if n % 8 == 2 and n > 8:
                            output(pr * 2 + (n - 8) // SLOTS, (n - 8) % SLOTS // 8)
                        elif n == 2 and not isinstance(pr, int):
                            output(pr * 2 - 1, NQB - 1)
                pair(0)
                with act.Fori(1, PAIRS) as pr:
                    pair(pr)
                output(HEADS - 1, NQB - 1)

            @block.tensor
            def _(pe):
                pe.wait_ge(s["fixed"], 10)

                def item(hh, kind, n, index, base, half):
                    pe.wait_ge(s["ring_free"], base * NI + (index + 1))
                    bank = ps_r[:, index % 2]
                    if kind in "KQ":
                        src, name = (kd, "kd") if kind == "K" else (qd, "qd")
                        if n == 0:
                            pe.wait_ge(s[f"{name}{hh}"], half * 32 + 32)
                        for t in range(4):
                            m = pe.transpose(bank[:, t * P:(t + 1) * P],
                                             src[:, hh, 4 * n + t].rearrange("p w c -> p (w c)"), ident)
                    elif kind == "U":
                        if n == 0:
                            pe.wait_ge(s["ring_free"], base * NI + 10)
                        t, kb = n // 4, n % 4
                        m = pe.matmul(bank, q1[hh][:, t * P:(t + 1) * P], k1[hh][:, kb * QB:(kb + 1) * QB],
                                      start=True, stop=True)
                    else:
                        pe.wait_ge(s["nm_ready"], base * NG + (n + 1))
                        for t in range(4):
                            m = pe.transpose(bank[0:1, t * P:(t + 1) * P], nm[:, 4 * n + t:4 * n + t + 1], ident)
                    m.then_inc(s["ring_full"], 1)

                def scores(g, hh, n, j):
                    if n >= SLOTS:
                        g, hh, n = g + 1, 1 - hh, n - SLOTS
                    qb, c2 = n // 8, n % 8
                    if j == 0:
                        pe.wait_ge(s["p_ready"], g * SLOTS + (n + 1))
                    if c2 == 0 and j == 0:
                        pe.wait_ge(s["q2_ready"], g * NG + (qb + 1))
                        if qb == 0:
                            pe.wait_ge(s["k_copied"], g * NG + NG)
                    c = 2 * c2 + j
                    ks, qs = slice(c * P, (c + 1) * P), slice(qb * QB, (qb + 1) * QB)
                    out = ps_s[:, n % 2, j * QB:(j + 1) * QB]
                    pe.matmul(out, k1[hh][:, ks], q1[hh][:, qs], start=True, stop=False)
                    m = pe.matmul(out, k2[hh][:, ks], q2[hh][:, qs], start=False, stop=True)
                    if j == 1:
                        m.then_inc(s["s_full"], 1)

                def values(g, hh, n, j):
                    qb, c2 = n // 8, n % 8
                    if j == 0:
                        if n == 0:
                            pe.wait_ge(s["v_split"], g + 1)
                        if c2 == 0:
                            pe.wait_ge(s["o_ready"], g * NQB + (qb + 1))
                        pe.wait_ge(s["pl_ready"], g * SLOTS + (n + 1))
                    elif n in SHARED:
                        pe.wait_ge(s["pl2_ready"], g * len(SHARED) + (SHARED.index(n) + 1))
                    c = 2 * c2 + j
                    out, keys = ps_v[:, qb % 2], slice(j * QB, (j + 1) * QB)
                    pe.matmul(out, vh[:, hh, c], ph[:, n % NP, keys], start=c == 0, stop=False)
                    pe.matmul(out, vl[:, hh, c], ph[:, n % NP, keys], start=False, stop=False)
                    m = pe.matmul(out, vh[:, hh, c], pl[:, n % NP, keys], start=False, stop=c == KC - 1)
                    if j == 1:
                        m.then_inc(s["pv_done"], 1)

                def head(pr, hh, prepare):
                    g, nxt = pr * 2 + hh, pr * 2 + (hh + 1)
                    index = 0
                    for n in range(SLOTS):
                        work = list(plan[n]) if prepare else []
                        for place in range(4):
                            if place < 2:
                                if n + 2 < SLOTS or prepare:
                                    scores(g, hh, n + 2, place)
                            else:
                                values(g, hh, n, place - 2)
                            if place > 0 and work:
                                item(1 - hh, *work.pop(0), index, nxt, pr + hh)
                                index += 1

                for index, (kind, m) in enumerate(items):
                    item(0, kind, m, index, 0, 0)
                for n in range(2):
                    for j in range(2):
                        scores(0, 0, n, j)
                with pe.Fori(0, PAIRS - 1) as pr:
                    head(pr, 0, True)
                    head(pr, 1, True)
                head(PAIRS - 1, 0, True)
                head(PAIRS - 1, 1, False)

    def output_projection(self):
        nc, ins, x = self.nc, self.ins, self.x
        ctx, sb, ps, sem = self.scope("op")
        G = H // 2
        with ctx:
            wo = sb("wo", [P, G, D])
            oT = sb("oT", [P, 4, G, P])
            rb = sb("rb", [P, 4, G, P])
            dn = sb("dn", [P, B * H * L // P])
            rd = sb("rd", [P, B * H * L // P])
            stats = sb("stats", [P, 6])
            agg = sb("agg", [P, 2])
            ps_o = ps("ps_o", [P, 2, 512])
            s = {n: sem(n) for n in "turns own x weights den recip rden o0 o1 o2 o3 norm_ready out_ready added".split()}
            block = ctx.enter_context(nc.Block())

            def flat(t):
                return t[:].rearrange("g h l -> (g h l)").rearrange("(p f) -> p f", p=P)

            @block.sync
            def _(sp):
                sp.dma_start(dn[:], flat(self.den)).then_inc(s["den"], 16)
                sp.dma_start(wo[:], ins["w_outT"].rearrange("(g p) n -> p g n", p=P)).then_inc(s["weights"], 16)
                sp.dma_start(x[:], self.x_acc[:].rearrange("(n p) d -> p n d", p=P)).then_inc(s["x"], 16)
                sp.wait_ge(s["recip"], 1)
                sp.dma_start(flat(self.rden), rd[:]).then_inc(s["rden"], 16)
                sp.wait_ge(s["rden"], 16)
                for b in range(B):
                    src = self.o_dram[b * G:(b + 1) * G].rearrange("g p (n l) -> p n g l", l=P)
                    rec = self.rden[b * G:(b + 1) * G].rearrange("g h (n l) -> h n g l", l=P)

                    def load(j, r):
                        sp.dma_start(oT[:, r], src[:, bass.ds(j + r, 1)].squeeze(1)).then_inc(s[f"o{r}"], 16)
                        for h in range(2):
                            sp.dma_start(rb[h * DH:(h + 1) * DH, r],
                                         rec[h, bass.ds(j + r, 1)].squeeze(0).partition_broadcast(DH))\
                                .then_inc(s[f"o{r}"], 16)
                    if b == 0:
                        for r in range(4):
                            load(0, r)
                    with sp.Fori(4 if b == 0 else 0, TB - 3, 4) as j:
                        for r in range(4):
                            sp.wait_ge(s["out_ready"], j + (b * TB - 4 + r + 1))
                            load(j, r)

            @block.tensor
            def _(pe):
                pe.wait_ge(s["weights"], 16)
                pe.sem_inc(s["added"], 2)
                with pe.Fori(0, NT - 3, 4) as j:
                    for r in range(4):
                        pe.wait_ge(s["norm_ready"], j + (r + 1))
                        pe.wait_ge(s["added"], j + (r + 1))
                        for g in range(G):
                            m = pe.matmul(ps_o[:, r % 2, 0:D], oT[:, r, g], wo[:, g], start=g == 0, stop=g == G - 1)
                        m.then_inc(s["out_ready"], 1)

            @block.vector
            def _(dve):
                own = Chain(dve, s["own"])
                dve.wait_ge(s["den"], 16)
                dve.reciprocal(rd[:], dn[:]).then_inc(s["recip"], 1)

                def normalise(i, r):
                    dve.wait_ge(s[f"o{r % 4}"], i * 12 + (48 - 12 * (r % 4)))
                    dve.tensor_tensor(oT[:, r % 4], oT[:, r % 4], rb[:, r % 4], ALU.mult).then_inc(s["norm_ready"], 1)

                def step(i, r):
                    if exists(i + 2, NT):
                        normalise(i + 2, r + 2)
                    dve.wait_ge(s["out_ready"], i + 1)
                    dve.tensor_tensor(x[:, bass.ds(i, 1)].squeeze(1), ps_o[:, r % 2, 0:D],
                                      x[:, bass.ds(i, 1)].squeeze(1), ALU.add).then_inc(s["added"], 1)
                    own.begin(i * 3)
                    dve.wait_ge(s["added"], i + 3)
                    stand_alone(dve, s["turns"])
                    own(dve.bn_stats(stats[:], x[:, bass.ds(i, 1)].squeeze(1)))
                    stand_alone(dve, s["turns"])
                    own(dve.bn_aggr(agg[:], stats[:]))
                    own(dve.tensor_copy(self.mv[:, bass.ds(i, 1), :].squeeze(1), agg[:]))

                def prologue():
                    for i in range(2):
                        normalise(i, i)
                    dve.wait_ge(s["x"], 16)
                pipeline(dve, NT, 4, prologue, step)

    def add_odd(self):
        nc = self.nc
        ctx, sb, ps, sem = self.scope("ao")
        QUARTERS = 4
        with ctx:
            even = sb("even", [P, NT, D])
            odd = sb("odd", [P, NT, D])
            s = {n: sem(n) for n in "in0 in1 in2 in3 added stored".split()}
            block = ctx.enter_context(nc.Block())

            def part(q, of=None):
                tiles = slice(q * NT // QUARTERS, (q + 1) * NT // QUARTERS)
                return tiles if of is None else of.rearrange("(n p) d -> p n d", p=P)[:, tiles]

            @block.sync
            def _(sp):
                for q in range(QUARTERS):
                    sp.dma_start(even[:, part(q)], part(q, self.out)).then_inc(s[f"in{q}"], 16)
                    sp.dma_start(odd[:, part(q)], part(q, self.out_odd[:])).then_inc(s[f"in{q}"], 16)
                for q in range(QUARTERS):
                    sp.wait_ge(s["added"], q + 1)
                    sp.dma_start(part(q, self.out), even[:, part(q)]).then_inc(s["stored"], 16)
                sp.wait_ge(s["stored"], 16 * QUARTERS)

            @block.vector
            def _(dve):
                for q in range(QUARTERS):
                    dve.wait_ge(s[f"in{q}"], 32)
                    dve.tensor_tensor(even[:, part(q)], even[:, part(q)], odd[:, part(q)], ALU.add)\
                        .then_inc(s["added"], 1)


def kernel(L0_attn_X, L0_attn_Wq, L0_attn_Wv, L0_attn_q_norm_w, L0_attn_v_norm_w, L0_ffn_Wg, L0_ffn_bg,
           L0_ffn_Wgu, L0_ffn_bgu, L0_ffn_Wd, L0_ffn_bd, L1_attn_w_down_q, L1_attn_w_down_kv, L1_attn_w_up_q,
           L1_attn_w_up_k, L1_attn_w_up_v, L1_attn_w_out, L1_attn_ln_scale, L1_attn_ln_bias, L1_ffn_gate_w,
           L1_ffn_w_gate, L1_ffn_w_up, L1_ffn_w_down):
    import concourse.bacc as bacc
    from concourse.bass_utils import run_bass_kernel_spmd

    def halves(w):
        w = np.asarray(w).reshape(H, HALF, 2, P).transpose(0, 2, 1, 3).reshape(H * DH, P)
        return w.T

    def deinterleave(w):
        w = np.asarray(w)
        return np.concatenate([w[..., ::2], w[..., 1::2]], -1)

    def ln_columns(v):
        return np.asarray(v).reshape(DC, P).T
    arrays = {
        "X": np.asarray(L0_attn_X).reshape(T, D),
        "consts": shape_constants(), "rope": rope_constants(),
        "WqT": np.asarray(L0_attn_Wq).T, "WvT": np.asarray(L0_attn_Wv).T,
        "qw": np.asarray(L0_attn_q_norm_w).reshape(-1), "vw": np.asarray(L0_attn_v_norm_w).reshape(-1),
        "router0": np.asarray(L0_ffn_Wg).T, "bg": np.asarray(L0_ffn_bg),
        "Wgu": deinterleave(L0_ffn_Wgu), "bgu": deinterleave(L0_ffn_bgu),
        "Wd": np.asarray(L0_ffn_Wd), "bd": np.asarray(L0_ffn_bd),
        "w_down_qT": np.asarray(L1_attn_w_down_q).T, "w_down_kvT": np.asarray(L1_attn_w_down_kv).T,
        "w_up_qT": halves(L1_attn_w_up_q), "w_up_kT": halves(L1_attn_w_up_k),
        "w_up_vT": np.asarray(L1_attn_w_up_v).T, "w_outT": np.asarray(L1_attn_w_out).T,
        "ln": np.stack([ln_columns(L1_attn_ln_scale), ln_columns(L1_attn_ln_bias)], -1),
        "router1": np.asarray(L1_ffn_gate_w).T,
        "Wgu1": np.concatenate([np.asarray(L1_ffn_w_gate), np.asarray(L1_ffn_w_up)], 1).transpose(0, 2, 1),
        "Wd1": np.asarray(L1_ffn_w_down).transpose(0, 2, 1),
    }
    arrays = {k: np.ascontiguousarray(v) for k, v in arrays.items()}
    nc = bacc.Bacc("TRN2", target_bir_lowering=False, num_devices=1)
    ins = {k: nc.dram_tensor(k + "_in", v.shape, mybir.dt.from_np(v.dtype), kind="ExternalInput").ap()
           for k, v in arrays.items()}
    out = nc.dram_tensor("out", (T, D), F32, kind="ExternalOutput").ap()
    Kernel(nc, ins, out).build()
    r = run_bass_kernel_spmd(nc, [{k + "_in": v for k, v in arrays.items()}], core_ids=[0])
    return r.results[0]["out"].reshape(B, L, D)
```
